# Optimizing a Trainium2 kernel written in Bass

```python
import numpy as np
import jax
import jax.numpy as jnp

def _softmax(x, axis=-1):
    return jax.nn.softmax(x, axis=axis)

def _gelu(x):
    return jax.nn.gelu(x, approximate=True)

def _silu(x):
    return jax.nn.silu(x)

def _sigmoid(x):
    return jax.nn.sigmoid(x)

def _layernorm(x, axis=-1, eps=1e-05):
    m = jnp.mean(x, axis=axis, keepdims=True)
    v = jnp.var(x, axis=axis, keepdims=True)
    return (x - m) / jnp.sqrt(v + eps)

def _scatter_add(tgt, idx, src, axis=0):
    return tgt.at[idx].add(src)

def _segment_sum(src, seg, n):
    return jax.ops.segment_sum(src, seg, n)
kernel_name = 'mk_rec_standalone_d1_rec_r8_a1731a'

def setup_inputs(seed: int=0):
    np.random.seed(seed)
    _w = jnp.asarray

    def _rec_inputs():
        import jax
        import jax.numpy as jnp
        _rk = jax.random.key(seed)
        r_items = jax.random.randint(jax.random.fold_in(_rk, 1), (512,), 72, 99964, jnp.int32)
        r_users = jax.random.randint(jax.random.fold_in(_rk, 2), (512,), 202, 499889, jnp.int32)
        r_history_users = jnp.stack([jax.random.randint(jax.random.fold_in(jax.random.fold_in(_rk, 3), 0), (512,), 160, 499921, jnp.int32), jax.random.randint(jax.random.fold_in(jax.random.fold_in(_rk, 3), 1), (512,), 19, 499891, jnp.int32), jax.random.randint(jax.random.fold_in(jax.random.fold_in(_rk, 3), 2), (512,), 168, 499845, jnp.int32), jax.random.randint(jax.random.fold_in(jax.random.fold_in(_rk, 3), 3), (512,), 72, 62493, jnp.int32), jax.random.randint(jax.random.fold_in(jax.random.fold_in(_rk, 3), 4), (512,), 170, 499705, jnp.int32), jax.random.randint(jax.random.fold_in(jax.random.fold_in(_rk, 3), 5), (512,), 134, 499997, jnp.int32), jax.random.randint(jax.random.fold_in(jax.random.fold_in(_rk, 3), 6), (512,), 238, 499951, jnp.int32), jax.random.randint(jax.random.fold_in(jax.random.fold_in(_rk, 3), 7), (512,), 10, 62498, jnp.int32), jax.random.randint(jax.random.fold_in(jax.random.fold_in(_rk, 3), 8), (512,), 17, 499937, jnp.int32), jax.random.randint(jax.random.fold_in(jax.random.fold_in(_rk, 3), 9), (512,), 115, 499916, jnp.int32), jax.random.randint(jax.random.fold_in(jax.random.fold_in(_rk, 3), 10), (512,), 53, 499815, jnp.int32), jax.random.randint(jax.random.fold_in(jax.random.fold_in(_rk, 3), 11), (512,), 99, 499978, jnp.int32), jax.random.randint(jax.random.fold_in(jax.random.fold_in(_rk, 3), 12), (512,), 31, 499838, jnp.int32), jax.random.randint(jax.random.fold_in(jax.random.fold_in(_rk, 3), 13), (512,), 32, 499929, jnp.int32), jax.random.randint(jax.random.fold_in(jax.random.fold_in(_rk, 3), 14), (512,), 36, 499830, jnp.int32), jax.random.randint(jax.random.fold_in(jax.random.fold_in(_rk, 3), 15), (512,), 75, 499843, jnp.int32), jax.random.randint(jax.random.fold_in(jax.random.fold_in(_rk, 3), 16), (512,), 70, 499867, jnp.int32), jax.random.randint(jax.random.fold_in(jax.random.fold_in(_rk, 3), 17), (512,), 305, 499902, jnp.int32), jax.random.randint(jax.random.fold_in(jax.random.fold_in(_rk, 3), 18), (512,), 59, 499846, jnp.int32), jax.random.randint(jax.random.fold_in(jax.random.fold_in(_rk, 3), 19), (512,), 3, 62456, jnp.int32), jax.random.randint(jax.random.fold_in(jax.random.fold_in(_rk, 3), 20), (512,), 325, 499879, jnp.int32), jax.random.randint(jax.random.fold_in(jax.random.fold_in(_rk, 3), 21), (512,), 53, 499841, jnp.int32), jax.random.randint(jax.random.fold_in(jax.random.fold_in(_rk, 3), 22), (512,), 125, 499977, jnp.int32), jax.random.randint(jax.random.fold_in(jax.random.fold_in(_rk, 3), 23), (512,), 224, 62451, jnp.int32), jax.random.randint(jax.random.fold_in(jax.random.fold_in(_rk, 3), 24), (512,), 320, 499637, jnp.int32), jax.random.randint(jax.random.fold_in(jax.random.fold_in(_rk, 3), 25), (512,), 1, 499932, jnp.int32), jax.random.randint(jax.random.fold_in(jax.random.fold_in(_rk, 3), 26), (512,), 90, 499882, jnp.int32), jax.random.randint(jax.random.fold_in(jax.random.fold_in(_rk, 3), 27), (512,), 86, 499915, jnp.int32), jax.random.randint(jax.random.fold_in(jax.random.fold_in(_rk, 3), 28), (512,), 62, 499940, jnp.int32), jax.random.randint(jax.random.fold_in(jax.random.fold_in(_rk, 3), 29), (512,), 18, 499965, jnp.int32), jax.random.randint(jax.random.fold_in(jax.random.fold_in(_rk, 3), 30), (512,), 128, 499966, jnp.int32), jax.random.randint(jax.random.fold_in(jax.random.fold_in(_rk, 3), 31), (512,), 36, 499690, jnp.int32), jax.random.randint(jax.random.fold_in(jax.random.fold_in(_rk, 3), 32), (512,), 92, 62495, jnp.int32), jax.random.randint(jax.random.fold_in(jax.random.fold_in(_rk, 3), 33), (512,), 247, 499771, jnp.int32), jax.random.randint(jax.random.fold_in(jax.random.fold_in(_rk, 3), 34), (512,), 77, 499954, jnp.int32), jax.random.randint(jax.random.fold_in(jax.random.fold_in(_rk, 3), 35), (512,), 253, 499908, jnp.int32), jax.random.randint(jax.random.fold_in(jax.random.fold_in(_rk, 3), 36), (512,), 45, 499651, jnp.int32), jax.random.randint(jax.random.fold_in(jax.random.fold_in(_rk, 3), 37), (512,), 303, 499854, jnp.int32), jax.random.randint(jax.random.fold_in(jax.random.fold_in(_rk, 3), 38), (512,), 146, 499980, jnp.int32), jax.random.randint(jax.random.fold_in(jax.random.fold_in(_rk, 3), 39), (512,), 559, 62460, jnp.int32), jax.random.randint(jax.random.fold_in(jax.random.fold_in(_rk, 3), 40), (512,), 101, 62471, jnp.int32), jax.random.randint(jax.random.fold_in(jax.random.fold_in(_rk, 3), 41), (512,), 184, 499862, jnp.int32), jax.random.randint(jax.random.fold_in(jax.random.fold_in(_rk, 3), 42), (512,), 68, 499997, jnp.int32), jax.random.randint(jax.random.fold_in(jax.random.fold_in(_rk, 3), 43), (512,), 107, 499970, jnp.int32), jax.random.randint(jax.random.fold_in(jax.random.fold_in(_rk, 3), 44), (512,), 17, 499893, jnp.int32), jax.random.randint(jax.random.fold_in(jax.random.fold_in(_rk, 3), 45), (512,), 384, 499387, jnp.int32), jax.random.randint(jax.random.fold_in(jax.random.fold_in(_rk, 3), 46), (512,), 113, 499743, jnp.int32), jax.random.randint(jax.random.fold_in(jax.random.fold_in(_rk, 3), 47), (512,), 497, 499855, jnp.int32), jax.random.randint(jax.random.fold_in(jax.random.fold_in(_rk, 3), 48), (512,), 50, 499761, jnp.int32), jax.random.randint(jax.random.fold_in(jax.random.fold_in(_rk, 3), 49), (512,), 11, 499910, jnp.int32), jax.random.randint(jax.random.fold_in(jax.random.fold_in(_rk, 3), 50), (512,), 71, 499946, jnp.int32), jax.random.randint(jax.random.fold_in(jax.random.fold_in(_rk, 3), 51), (512,), 14, 499970, jnp.int32), jax.random.randint(jax.random.fold_in(jax.random.fold_in(_rk, 3), 52), (512,), 38, 499931, jnp.int32), jax.random.randint(jax.random.fold_in(jax.random.fold_in(_rk, 3), 53), (512,), 136, 499836, jnp.int32), jax.random.randint(jax.random.fold_in(jax.random.fold_in(_rk, 3), 54), (512,), 39, 499868, jnp.int32), jax.random.randint(jax.random.fold_in(jax.random.fold_in(_rk, 3), 55), (512,), 233, 499989, jnp.int32), jax.random.randint(jax.random.fold_in(jax.random.fold_in(_rk, 3), 56), (512,), 66, 499854, jnp.int32), jax.random.randint(jax.random.fold_in(jax.random.fold_in(_rk, 3), 57), (512,), 34, 499969, jnp.int32), jax.random.randint(jax.random.fold_in(jax.random.fold_in(_rk, 3), 58), (512,), 17, 62496, jnp.int32), jax.random.randint(jax.random.fold_in(jax.random.fold_in(_rk, 3), 59), (512,), 459, 499807, jnp.int32), jax.random.randint(jax.random.fold_in(jax.random.fold_in(_rk, 3), 60), (512,), 11, 62498, jnp.int32), jax.random.randint(jax.random.fold_in(jax.random.fold_in(_rk, 3), 61), (512,), 4, 499901, jnp.int32), jax.random.randint(jax.random.fold_in(jax.random.fold_in(_rk, 3), 62), (512,), 41, 499899, jnp.int32), jax.random.randint(jax.random.fold_in(jax.random.fold_in(_rk, 3), 63), (512,), 153, 499995, jnp.int32), jax.random.randint(jax.random.fold_in(jax.random.fold_in(_rk, 3), 64), (512,), 68, 499908, jnp.int32), jax.random.randint(jax.random.fold_in(jax.random.fold_in(_rk, 3), 65), (512,), 138, 499947, jnp.int32), jax.random.randint(jax.random.fold_in(jax.random.fold_in(_rk, 3), 66), (512,), 23, 62494, jnp.int32), jax.random.randint(jax.random.fold_in(jax.random.fold_in(_rk, 3), 67), (512,), 91, 62495, jnp.int32), jax.random.randint(jax.random.fold_in(jax.random.fold_in(_rk, 3), 68), (512,), 43, 499807, jnp.int32), jax.random.randint(jax.random.fold_in(jax.random.fold_in(_rk, 3), 69), (512,), 30, 499942, jnp.int32), jax.random.randint(jax.random.fold_in(jax.random.fold_in(_rk, 3), 70), (512,), 18, 499964, jnp.int32), jax.random.randint(jax.random.fold_in(jax.random.fold_in(_rk, 3), 71), (512,), 2, 499926, jnp.int32), jax.random.randint(jax.random.fold_in(jax.random.fold_in(_rk, 3), 72), (512,), 29, 499971, jnp.int32), jax.random.randint(jax.random.fold_in(jax.random.fold_in(_rk, 3), 73), (512,), 143, 499701, jnp.int32), jax.random.randint(jax.random.fold_in(jax.random.fold_in(_rk, 3), 74), (512,), 7, 499981, jnp.int32), jax.random.randint(jax.random.fold_in(jax.random.fold_in(_rk, 3), 75), (512,), 82, 62482, jnp.int32), jax.random.randint(jax.random.fold_in(jax.random.fold_in(_rk, 3), 76), (512,), 30, 499674, jnp.int32), jax.random.randint(jax.random.fold_in(jax.random.fold_in(_rk, 3), 77), (512,), 63, 499931, jnp.int32), jax.random.randint(jax.random.fold_in(jax.random.fold_in(_rk, 3), 78), (512,), 135, 499949, jnp.int32), jax.random.randint(jax.random.fold_in(jax.random.fold_in(_rk, 3), 79), (512,), 313, 62499, jnp.int32), jax.random.randint(jax.random.fold_in(jax.random.fold_in(_rk, 3), 80), (512,), 286, 499854, jnp.int32), jax.random.randint(jax.random.fold_in(jax.random.fold_in(_rk, 3), 81), (512,), 17, 499994, jnp.int32), jax.random.randint(jax.random.fold_in(jax.random.fold_in(_rk, 3), 82), (512,), 14, 499967, jnp.int32), jax.random.randint(jax.random.fold_in(jax.random.fold_in(_rk, 3), 83), (512,), 16, 499931, jnp.int32), jax.random.randint(jax.random.fold_in(jax.random.fold_in(_rk, 3), 84), (512,), 59, 499907, jnp.int32), jax.random.randint(jax.random.fold_in(jax.random.fold_in(_rk, 3), 85), (512,), 458, 499979, jnp.int32), jax.random.randint(jax.random.fold_in(jax.random.fold_in(_rk, 3), 86), (512,), 75, 499939, jnp.int32), jax.random.randint(jax.random.fold_in(jax.random.fold_in(_rk, 3), 87), (512,), 61, 499963, jnp.int32), jax.random.randint(jax.random.fold_in(jax.random.fold_in(_rk, 3), 88), (512,), 269, 62489, jnp.int32), jax.random.randint(jax.random.fold_in(jax.random.fold_in(_rk, 3), 89), (512,), 80, 62496, jnp.int32), jax.random.randint(jax.random.fold_in(jax.random.fold_in(_rk, 3), 90), (512,), 11, 62476, jnp.int32), jax.random.randint(jax.random.fold_in(jax.random.fold_in(_rk, 3), 91), (512,), 196, 499958, jnp.int32), jax.random.randint(jax.random.fold_in(jax.random.fold_in(_rk, 3), 92), (512,), 23, 499930, jnp.int32), jax.random.randint(jax.random.fold_in(jax.random.fold_in(_rk, 3), 93), (512,), 295, 499626, jnp.int32), jax.random.randint(jax.random.fold_in(jax.random.fold_in(_rk, 3), 94), (512,), 97, 499934, jnp.int32), jax.random.randint(jax.random.fold_in(jax.random.fold_in(_rk, 3), 95), (512,), 157, 499937, jnp.int32), jax.random.randint(jax.random.fold_in(jax.random.fold_in(_rk, 3), 96), (512,), 24, 499978, jnp.int32), jax.random.randint(jax.random.fold_in(jax.random.fold_in(_rk, 3), 97), (512,), 124, 499977, jnp.int32), jax.random.randint(jax.random.fold_in(jax.random.fold_in(_rk, 3), 98), (512,), 71, 499858, jnp.int32), jax.random.randint(jax.random.fold_in(jax.random.fold_in(_rk, 3), 99), (512,), 124, 499967, jnp.int32)], axis=1)
        return (r_items, r_users, r_history_users)
    r_items, r_users, r_history_users = _rec_inputs()

    def _L0_rec_setup():
        import jax, jax.numpy as jnp
        import numpy as np
        B, H, D = (512, 100, 128)
        N_ITEM, M_USER = (12500, 62500)
        D_IN, D1, D2 = (3 * D, 1024, 512)
        DICE_EPS = 0.001
        BN_EPS = 1e-05

        def _xavier(key, shape):
            fan_in, fan_out = (shape[0], shape[1])
            lim = jnp.sqrt(6.0 / (fan_in + fan_out))
            return jax.random.uniform(key, shape, jnp.float32, -lim, lim)

        def _dice(x, alpha):
            avg = x.mean(axis=1, keepdims=True)
            var = jnp.sum((x - avg) ** 2 + DICE_EPS, axis=1, keepdims=True)
            ps = jax.nn.sigmoid((x - avg) / jnp.sqrt(var))
            return ps * x + (1.0 - ps) * alpha * x

        def _batchnorm(x, gamma, beta):
            mu = x.mean(axis=0, keepdims=True)
            var = x.var(axis=0, keepdims=True)
            return (x - mu) / jnp.sqrt(var + BN_EPS) * gamma + beta
        key = jax.random.key(seed)
        ks = jax.random.split(key, 12)
        return {'items': jax.random.randint(ks[0], (B,), 0, N_ITEM), 'users': jax.random.randint(ks[1], (B,), 0, M_USER), 'history_users': jax.random.randint(ks[2], (B, H), 0, M_USER), 'item_table': _xavier(ks[3], (N_ITEM, D)), 'user_table': _xavier(ks[4], (M_USER, D)), 'W1': _xavier(ks[5], (D_IN, D1)), 'b1': jnp.zeros((D1,), jnp.float32), 'g1': jnp.ones((D1,), jnp.float32), 'be1': jnp.zeros((D1,), jnp.float32), 'a1': jax.random.normal(ks[6], (1,), jnp.float32), 'W2': _xavier(ks[7], (D1, D2)), 'b2': jnp.zeros((D2,), jnp.float32), 'g2': jnp.ones((D2,), jnp.float32), 'be2': jnp.zeros((D2,), jnp.float32), 'a2': jax.random.normal(ks[8], (1,), jnp.float32), 'W3': _xavier(ks[9], (D2, 1)), 'b3': jnp.zeros((1,), jnp.float32)}
    _L0_rec_all = _L0_rec_setup()
    _L0_rec_in = {k: v for k, v in _L0_rec_all.items() if k in ('item_table', 'user_table', 'W1', 'b1', 'g1', 'be1', 'a1', 'W2', 'b2', 'g2', 'be2', 'a2', 'W3', 'b3')}
    del _L0_rec_all
    return {'r_items': r_items, 'r_users': r_users, 'r_history_users': r_history_users, 'L0_rec_item_table': _L0_rec_in['item_table'], 'L0_rec_user_table': _L0_rec_in['user_table'], 'L0_rec_W1': _L0_rec_in['W1'], 'L0_rec_b1': _L0_rec_in['b1'], 'L0_rec_g1': _L0_rec_in['g1'], 'L0_rec_be1': _L0_rec_in['be1'], 'L0_rec_a1': _L0_rec_in['a1'], 'L0_rec_W2': _L0_rec_in['W2'], 'L0_rec_b2': _L0_rec_in['b2'], 'L0_rec_g2': _L0_rec_in['g2'], 'L0_rec_be2': _L0_rec_in['be2'], 'L0_rec_a2': _L0_rec_in['a2'], 'L0_rec_W3': _L0_rec_in['W3'], 'L0_rec_b3': _L0_rec_in['b3']}

def reference(r_items, r_users, r_history_users, L0_rec_item_table, L0_rec_user_table, L0_rec_W1, L0_rec_b1, L0_rec_g1, L0_rec_be1, L0_rec_a1, L0_rec_W2, L0_rec_b2, L0_rec_g2, L0_rec_be2, L0_rec_a2, L0_rec_W3, L0_rec_b3):
    import jax
    import jax.numpy as jnp

    def _L0_rec_ref(items, users, history_users, item_table, user_table, W1, b1, g1, be1, a1, W2, b2, g2, be2, a2, W3, b3):
        import jax, jax.numpy as jnp
        import numpy as np
        B, H, D = (512, 100, 128)
        N_ITEM, M_USER = (12500, 62500)
        D_IN, D1, D2 = (3 * D, 1024, 512)
        DICE_EPS = 0.001
        BN_EPS = 1e-05

        def _xavier(key, shape):
            fan_in, fan_out = (shape[0], shape[1])
            lim = jnp.sqrt(6.0 / (fan_in + fan_out))
            return jax.random.uniform(key, shape, jnp.float32, -lim, lim)

        def _dice(x, alpha):
            avg = x.mean(axis=1, keepdims=True)
            var = jnp.sum((x - avg) ** 2 + DICE_EPS, axis=1, keepdims=True)
            ps = jax.nn.sigmoid((x - avg) / jnp.sqrt(var))
            return ps * x + (1.0 - ps) * alpha * x

        def _batchnorm(x, gamma, beta):
            mu = x.mean(axis=0, keepdims=True)
            var = x.var(axis=0, keepdims=True)
            return (x - mu) / jnp.sqrt(var + BN_EPS) * gamma + beta
        items_emb = item_table[items]
        user_emb = user_table[users]
        hist_emb = user_table[history_users]
        scores = jnp.einsum('bhd,bd->bh', hist_emb, user_emb)
        user_his_emb = jnp.einsum('bh,bhd->bd', scores, hist_emb)
        x = jnp.concatenate([items_emb, user_his_emb, user_emb], axis=1)
        x = _dice(_batchnorm(x @ W1 + b1, g1, be1), a1)
        x = _dice(_batchnorm(x @ W2 + b2, g2, be2), a2)
        return x @ W3 + b3
    y = _L0_rec_ref(r_items, r_users, r_history_users, L0_rec_item_table, L0_rec_user_table, L0_rec_W1, L0_rec_b1, L0_rec_g1, L0_rec_be1, L0_rec_a1, L0_rec_W2, L0_rec_b2, L0_rec_g2, L0_rec_be2, L0_rec_a2, L0_rec_W3, L0_rec_b3)
    return y

_drawn_inputs = setup_inputs


def setup_inputs(seed=0):
    import zlib

    import numpy as np

    out = dict(_drawn_inputs(seed))
    spreads = {'L0_rec_b1': (0.0, 0.8),
     'L0_rec_g1': (1.0, 0.2),
     'L0_rec_be1': (0.0, 0.8),
     'L0_rec_b2': (0.0, 0.8),
     'L0_rec_g2': (1.0, 0.2),
     'L0_rec_be2': (0.0, 0.293)}
    factors = {}
    for name, (base, spread) in spreads.items():
        noise = np.random.default_rng([zlib.crc32(name.encode()), seed]).standard_normal(out[name].shape)
        drawn = base * np.exp(spread * noise) if base else spread * noise
        out[name] = jnp.asarray(drawn.astype(out[name].dtype))
    for name, factor in factors.items():
        out[name] = (out[name] * factor).astype(out[name].dtype)
    return out
```

```python
from contextlib import ExitStack

import concourse.bass as bass
from concourse import mybir

F32 = mybir.dt.float32
I32 = mybir.dt.int32
ALU = mybir.AluOpType
ACT = mybir.ActivationFunctionType
AX = mybir.AxisListType

P = 128
QUARTER = 4
RING = 16
GROUP = 8
QUARTERS = RING // QUARTER
DICE_EPS = 1e-3
BN_EPS = 1e-5


def recommender_kernel(nc, items, users, history, item_table, user_table, W1, b1, g1, be1, a1,
                       W2, b2, g2, be2, a2, W3, b3, out):
    B, H = history.shape
    n_item, D = item_table.shape
    n_user = user_table.shape[0]
    d_in, F1 = W1.shape
    F2 = W2.shape[1]
    T = B // P
    M1, M2 = F1 // P, F2 // P
    KIN = d_in // P
    ITEMS, HIS, USER = range(KIN)
    HALF = M1 // 2
    PAD = -(-H // GROUP) * GROUP
    LOOPS = -(-H // RING)
    VEC = 3 * M1 + 3 * M2
    assert D == P and KIN == 3 and HALF * P == 512 and F2 == 512 and T == 4

    with ExitStack() as ctx:
        def sb(name, shape, dt=F32):
            return ctx.enter_context(nc.sbuf_tensor(name, shape, dt))

        def sem(name):
            return ctx.enter_context(nc.semaphore(name))

        bank = [ctx.enter_context(nc.psum_tensor(f"bank{i}", [P, 512], F32)) for i in range(8)]

        raw_users, raw_items = sb("raw_users", [P, T], I32), sb("raw_items", [P, T], I32)
        raw_history = sb("raw_history", [P, T, H], I32)
        wrap_u, wrap_i = sb("wrap_u", [P, T]), sb("wrap_i", [P, T])
        wrap_h = sb("wrap_h", [P, T, H])
        user_rows, item_rows = sb("user_rows", [P, T], I32), sb("item_rows", [P, T], I32)
        keys = sb("keys", [P, T, PAD])
        used = sb("used", [P, T, PAD])
        n_used, n_last = sb("n_used", [P, T]), sb("n_last", [P, T])
        needed = sb("needed", [T, 1], I32)
        top = sb("top", [P, T, 2, GROUP])
        slot_mask = sb("slot_mask", [P, T, 2, GROUP])
        slot_row = sb("slot_row", [P, T, 2, GROUP], I32)
        user_emb, item_emb = sb("user_emb", [P, T, D]), sb("item_emb", [P, T, D])
        ring = sb("ring", [P, 2, RING, D])
        last_row = sb("last_row", [P, D])
        product = sb("product", [P, 2, RING, D])
        last_product = sb("last_product", [P, T, D])
        score = sb("score", [P, T, RING])
        last_score = sb("last_score", [P, T])
        diag = sb("diag", [P, 2, RING, P])
        last_diag = sb("last_diag", [P, P])
        ident, zeros = sb("ident", [P, P]), sb("zeros", [P, P])
        minus_half = sb("minus_half", [P, M1])
        w1, w2 = sb("w1", [P, KIN, F1]), sb("w2", [P, M1, F2])
        w3 = sb("w3", [P, F2])
        vec_rows, vec = sb("vec_rows", [VEC, P]), sb("vec", [P, VEC])
        scalars, one_minus = sb("scalars", [P, 3]), sb("one_minus", [P, 2])
        xT = sb("xT", [P, KIN, B])
        y1 = sb("y1", [P, M1, B])
        stats1 = sb("stats1", [P, M1, T, 6])
        sig1 = sb("sig1", [P, 2, F1])
        x2 = sb("x2", [P, 2, F1])
        x2T = sb("x2T", [P, T, M1, P])
        y2 = sb("y2", [P, M2, B])
        stats2 = sb("stats2", [P, M2, T, 6])
        sig2, zw = sb("sig2", [P, T, F2]), sb("zw", [P, T, F2])
        bn = sb("bn", [P, 12, M1])
        bn_dev, bn_sq = sb("bn_dev", [P, M1, 2 * T]), sb("bn_sq", [P, M1, 2 * T])
        dice_stats = sb("dice_stats", [P, T, 12])
        dice_mv, dice_var = sb("dice_mv", [P, T, 2]), sb("dice_var", [P, T])
        dice_r, dice_nb = sb("dice_r", [P, T]), sb("dice_nb", [P, T])
        dice2_stats, dice2_mv = sb("dice2_stats", [P, T, 6]), sb("dice2_mv", [P, T, 2])
        dice2_var, dice2_r = sb("dice2_var", [P, T]), sb("dice2_r", [P, T])
        dice2_nb = sb("dice2_nb", [P, T])
        trash = sb("trash", [P, T, F2])
        plain, gated = sb("plain", [P, T]), sb("gated", [P, T])
        result = sb("result", [P, T])

        b1v, g1v, be1v = (vec[:, i * M1:(i + 1) * M1] for i in range(3))
        b2v, g2v, be2v = (vec[:, 3 * M1 + i * M2:3 * M1 + (i + 1) * M2] for i in range(3))
        alpha1, alpha2, bias3 = (scalars[:, i:i + 1] for i in range(3))

        users_loaded, items_loaded = sem("users_loaded"), sem("items_loaded")
        history_loaded, last_row_loaded = sem("history_loaded"), sem("last_row_loaded")
        vectors_loaded, w1_loaded, w2_loaded = sem("vectors_loaded"), sem("w1_loaded"), sem("w2_loaded")
        w3_loaded, scalars_loaded = sem("w3_loaded"), sem("scalars_loaded")
        zeros_set, ident_set, halves_set = sem("zeros_set"), sem("ident_set"), sem("halves_set")
        dve_step = sem("dve_step")
        user_rows_ready, item_rows_ready = sem("user_rows_ready"), sem("item_rows_ready")
        used_counted, counts_turned = sem("used_counted"), sem("counts_turned")
        needed_ready = sem("needed_ready")
        user_landed = [sem(f"user_landed{t}") for t in range(T)]
        item_landed = [sem(f"item_landed{t}") for t in range(T)]
        embs_turned, embs_copied = sem("embs_turned"), sem("embs_copied")
        vectors_turned, vec_ready = sem("vectors_turned"), sem("vec_ready")
        top_found = [sem(f"top_found{t}") for t in range(T)]
        keys_cut = [sem(f"keys_cut{t}") for t in range(T)]
        mask_ready = [sem(f"mask_ready{t}") for t in range(T)]
        rows_ready = [sem(f"rows_ready{t}") for t in range(T)]
        landed = [[sem(f"landed{t}_{q}") for q in range(QUARTERS)] for t in range(T)]
        scored = [sem(f"scored{t}") for t in range(T)]
        last_scored = sem("last_scored")
        diag_ready = [sem(f"diag_ready{t}") for t in range(T)]
        last_diag_ready = sem("last_diag_ready")
        ring_free = [sem(f"ring_free{t}") for t in range(T)]
        his_summed, his_copied = sem("his_summed"), sem("his_copied")
        gathering, sorting = sem("gathering"), sem("sorting")
        y1_summed, y1_copied = sem("y1_summed"), sem("y1_copied")
        var1_ready, rstd1_ready, affine1_ready = sem("var1_ready"), sem("rstd1_ready"), sem("affine1_ready")
        z1_by_act, z1_by_dve = sem("z1_by_act"), sem("z1_by_dve")
        z1_turned, dice_var_ready, dice_r_ready = sem("z1_turned"), sem("dice_var_ready"), sem("dice_r_ready")
        dice_nb_ready, sig1_ready, x2_ready = sem("dice_nb_ready"), sem("sig1_ready"), sem("x2_ready")
        x2_turned_low, x2_turned = sem("x2_turned_low"), sem("x2_turned")
        x2T_by_act, x2T_by_dve = sem("x2T_by_act"), sem("x2T_by_dve")
        y2_summed, y2_copied, y2_measured = sem("y2_summed"), sem("y2_copied"), sem("y2_measured")
        var2_ready, rstd2_ready, z2_ready = sem("var2_ready"), sem("rstd2_ready"), sem("z2_ready")
        z2_turned, dice2_var_ready, dice2_r_ready = sem("z2_turned"), sem("dice2_var_ready"), sem("dice2_r_ready")
        dice2_nb_ready, sig2_ready, zw_ready = sem("dice2_nb_ready"), sem("sig2_ready"), sem("zw_ready")
        result_ready, stored = sem("result_ready"), sem("stored")

        his_bank = [bank[0], bank[1]]
        y1_bank = [(bank[2], bank[3]), (bank[4], bank[5])]
        turn_items, turn_users = bank[6], bank[7]
        z1_bank = [(0, 1), (2, 3)]
        x2_bank = (4, 5)
        y2_bank = [bank[6], bank[7]]
        z2_bank = [bank[0], bank[1], bank[2], bank[3]]

        block = ctx.enter_context(nc.Block())

        @block.sync
        def _(sp):
            sp.dma_start(raw_users[:], users.rearrange("(p t) -> p t", t=T)).then_inc(users_loaded, 16)
            sp.dma_start(raw_history[:], history.rearrange("(p t) h -> p t h", t=T)).then_inc(history_loaded, 16)
            sp.dma_start(raw_items[:], items.rearrange("(p t) -> p t", t=T)).then_inc(items_loaded, 16)
            sp.dma_start(last_row[:], user_table[n_user - 1, :].partition_broadcast(P)).then_inc(last_row_loaded, 16)
            row = 0
            for v in (b1, g1, be1, b2, g2, be2):
                n = v.shape[0] // P
                sp.dma_start(vec_rows[row:row + n, :], v.rearrange("(m p) -> m p", p=P)).then_inc(vectors_loaded, 16)
                row += n
            sp.dma_start(w1[:], W1.rearrange("(k p) f -> p k f", p=P)).then_inc(w1_loaded, 16)
            sp.dma_start(w2[:], W2.rearrange("(k p) f -> p k f", p=P)).then_inc(w2_loaded, 16)
            sp.dma_start(w3[:], W3.rearrange("f o -> (f o)").partition_broadcast(P)).then_inc(w3_loaded, 16)
            for i, v in enumerate((a1, a2, b3)):
                sp.dma_start(scalars[:, i:i + 1], v.partition_broadcast(P)).then_inc(scalars_loaded, 16)
            sp.wait_ge(result_ready, 1)
            sp.dma_start(out.rearrange("(p t) o -> p (t o)", t=T), result[:]).then_inc(stored, 16)
            sp.wait_ge(stored, 16)

        @block.gpsimd
        def _(pool):
            pool.wait_ge(zeros_set, 1)
            nc.gpsimd.affine_select(out=ident[:], in_=zeros[:], compare_op=ALU.not_equal, fill=1.0, base=0,
                                    pattern=[[-1, P]], channel_multiplier=1).then_inc(ident_set, 1)

            def gather(dst, table, rows):
                return nc.gpsimd.indirect_dma_start(dst, None, table[:, :],
                                                    bass.IndirectOffsetOnAxis(ap=rows, axis=0))

            pool.wait_ge(user_rows_ready, 1)
            for t in range(T):
                gather(user_emb[:, t, :], user_table, user_rows[:, t:t + 1]).then_inc(user_landed[t], 16)
            pool.wait_ge(item_rows_ready, 1)
            for t in range(T):
                gather(item_emb[:, t, :], item_table, item_rows[:, t:t + 1]).then_inc(item_landed[t], 16)

            pool.wait_ge(needed_ready, 1)
            for t in range(T):
                par = t % 2
                need = pool.value_load(needed[t:t + 1, 0:1], min_val=0, max_val=H)

                def quarter(i, q):
                    group = q * QUARTER // GROUP
                    pool.wait_ge(rows_ready[t], 2 * i + group + 1)
                    pool.wait_ge(ring_free[t], QUARTERS * i + q + 1)
                    pool.sem_inc(gathering, 1)
                    for s in range(q * QUARTER, (q + 1) * QUARTER):
                        gather(ring[:, par, s, :], user_table,
                               slot_row[:, t, group, s % GROUP:s % GROUP + 1]).then_inc(landed[t][q], 16)

                with pool.Fori(0, LOOPS) as i:
                    for q in range(QUARTERS):
                        with pool.If(need > RING * i + QUARTER * q):
                            quarter(i, q)

            def rsqrt(dst, src, n):
                return nc.gpsimd.tensor_tensor(dst, src, minus_half[:, 0:n], ALU.pow)

            pool.wait_ge(halves_set, 1)
            pool.wait_ge(var1_ready, 1)
            rsqrt(bn[:, 3, :], bn[:, 2, :], M1).then_inc(rstd1_ready, 1)
            for t in range(T):
                pool.wait_ge(dice_var_ready, t + 1)
                rsqrt(dice_r[:, t:t + 1], dice_var[:, t:t + 1], 1).then_inc(dice_r_ready, 1)
            pool.wait_ge(var2_ready, 1)
            rsqrt(bn[:, 9, 0:M2], bn[:, 8, 0:M2], M2).then_inc(rstd2_ready, 1)
            pool.wait_ge(dice2_var_ready, 1)
            rsqrt(dice2_r[:], dice2_var[:], T).then_inc(dice2_r_ready, 1)

        @block.vector
        def _(dve):
            steps = [0]

            def step(ins):
                steps[0] += 1
                ins.then_inc(dve_step, 1)
                dve.wait_ge(dve_step, steps[0])

            nc.vector.memset(zeros[:], 0.0).then_inc(zeros_set, 1)
            nc.vector.memset(minus_half[:], -0.5).then_inc(halves_set, 1)
            step(nc.vector.memset(keys[:], 0.0))

            def clamp(raw, wrap, n):
                step(nc.vector.tensor_scalar(wrap, raw, 0.0, float(n), ALU.is_lt, ALU.mult))
                step(nc.vector.tensor_tensor(wrap, raw, wrap, ALU.add))
                step(nc.vector.tensor_scalar(wrap, wrap, 0.0, -1.0, ALU.max, ALU.mult))

            dve.wait_ge(users_loaded, 16)
            clamp(raw_users[:], wrap_u[:], n_user)
            step(nc.vector.tensor_scalar(wrap_u[:], wrap_u[:], float(n_user - 1), 0.0, ALU.add, ALU.max))
            nc.vector.tensor_scalar(user_rows[:], wrap_u[:], -1.0, float(n_user - 1),
                                    ALU.mult, ALU.add).then_inc(user_rows_ready, 1)
            dve.wait_ge(items_loaded, 16)
            clamp(raw_items[:], wrap_i[:], n_item)
            step(nc.vector.tensor_scalar(wrap_i[:], wrap_i[:], float(n_item - 1), 0.0, ALU.add, ALU.max))
            nc.vector.tensor_scalar(item_rows[:], wrap_i[:], -1.0, float(n_item - 1),
                                    ALU.mult, ALU.add).then_inc(item_rows_ready, 1)
            dve.wait_ge(history_loaded, 16)
            clamp(raw_history[:], wrap_h[:], n_user)
            step(nc.vector.tensor_scalar(keys[:, :, 0:H], wrap_h[:], float(n_user - 1), 0.0, ALU.add, ALU.max))
            step(nc.vector.tensor_scalar(used[:], keys[:], 1.0, None, ALU.min))
            nc.vector.tensor_reduce(n_used[:], used[:], AX.X, ALU.add).then_inc(used_counted, 1)

            def sort(t, group, n):
                par = t % 2
                dve.wait_ge(keys_cut[t], n)
                dve.sem_inc(sorting, 1)
                nc.vector.max(top[:, t, group, :], keys[:, t, :]).then_inc(top_found[t], 1)
                dve.wait_ge(top_found[t], n + 1)
                nc.vector.tensor_scalar(slot_row[:, t, group, :], top[:, t, group, :], -1.0,
                                        float(n_user - 1), ALU.mult, ALU.add).then_inc(rows_ready[t], 1)
                nc.vector.tensor_scalar(slot_mask[:, t, group, :], top[:, t, group, :], 1.0, None,
                                        ALU.min).then_inc(mask_ready[t], 1)
                nc.vector.match_replace(keys[:, t, :], top[:, t, group, :], keys[:, t, :],
                                        0.0).then_inc(keys_cut[t], 1)

            def first_sorts(t):
                par = t % 2
                nc.vector.max(top[:, t, 0, :], keys[:, t, :]).then_inc(top_found[t], 1)
                dve.wait_ge(top_found[t], 1)
                nc.vector.tensor_scalar(slot_row[:, t, 0, :], top[:, t, 0, :], -1.0,
                                        float(n_user - 1), ALU.mult, ALU.add).then_inc(rows_ready[t], 1)
                nc.vector.tensor_scalar(slot_mask[:, t, 0, :], top[:, t, 0, :], 1.0, None,
                                        ALU.min).then_inc(mask_ready[t], 1)
                nc.vector.match_replace(keys[:, t, :], top[:, t, 0, :], keys[:, t, :],
                                        0.0).then_inc(keys_cut[t], 1)
                sort(t, 1, 1)

            dve.wait_ge(counts_turned, 1)
            nc.vector.tensor_reduce(needed[:], bank[0][0:T, 0:P], AX.X, ALU.max).then_inc(needed_ready, 1)
            step(nc.vector.tensor_scalar(n_last[:], n_used[:], -1.0, float(H), ALU.mult, ALU.add))
            first_sorts(0)
            dve.wait_ge(scalars_loaded, 48)
            nc.vector.tensor_scalar(one_minus[:], scalars[:, 0:2], -1.0, 1.0, ALU.mult, ALU.add)
            dve.wait_ge(vectors_turned, 1)
            nc.vector.tensor_copy(vec[:], bank[1][:, 0:VEC]).then_inc(vec_ready, 1)
            dve.wait_ge(last_row_loaded, 16)
            dve.wait_ge(needed_ready, 1)

            def measure1(t):
                dve.wait_ge(y1_copied, t + 1)
                for m in range(M1):
                    last = nc.vector.bn_stats(stats1[:, m, t, :], y1[:, m, t * P:(t + 1) * P])
                return last

            for t in range(T):
                par = t % 2
                need = dve.value_load(needed[t:t + 1, 0:1], min_val=0, max_val=H)
                dve.wait_ge(user_landed[t], 16)
                nc.vector.tensor_tensor_reduce(last_product[:, t, :], last_row[:], user_emb[:, t, :], n_last[:, t:t + 1],
                                               0.0, ALU.mult, ALU.add,
                                               last_score[:, t:t + 1]).then_inc(last_scored, 1)
                if t + 1 < T:
                    first_sorts(t + 1)
                if t:
                    measure1(t - 1)

                def quarter(i, q):
                    group = q * QUARTER // GROUP
                    dve.wait_ge(mask_ready[t], 2 * i + group + 1)
                    dve.wait_ge(landed[t][q], 16 * QUARTER * (i + 1))
                    for s in range(q * QUARTER, (q + 1) * QUARTER):
                        last = nc.vector.tensor_tensor_reduce(
                            product[:, par, s, :], ring[:, par, s, :], user_emb[:, t, :],
                            slot_mask[:, t, group, s % GROUP:s % GROUP + 1], 0.0, ALU.mult, ALU.add,
                            score[:, t, s:s + 1])
                    last.then_inc(scored[t], 1)

                with dve.Fori(0, LOOPS) as i:
                    for q in range(QUARTERS):
                        with dve.If(need > RING * i + QUARTER * q):
                            quarter(i, q)
                        if q % 2:
                            with dve.If(need > RING * (i + 1) + GROUP * (q // 2)):
                                sort(t, q // 2, 2 * i + 2 + q // 2)

            step(measure1(T - 1))

            def batch_norm(stats, M, base, var_ready, rstd_ready, bias, gain, shift):
                groups = stats.rearrange("p m t (e c) -> p m (t e) c", e=2)
                mean, m2 = groups[:, :, :, 1], groups[:, :, :, 2]
                row = lambda n: bn[:, base + n, 0:M]
                dev, sq = bn_dev[:, 0:M, :], bn_sq[:, 0:M, :]
                step(nc.vector.tensor_reduce(row(0), mean, AX.X, ALU.add))
                step(nc.vector.tensor_scalar(row(0), row(0), 1.0 / (2 * T), None, ALU.mult))
                step(nc.vector.tensor_tensor(dev, mean, row(0).unsqueeze(2).to_broadcast([P, M, 2 * T]),
                                             ALU.subtract))
                step(nc.vector.tensor_tensor(sq, dev, dev, ALU.mult))
                nc.vector.tensor_reduce(row(1), sq, AX.X, ALU.add)
                step(nc.vector.tensor_reduce(row(2), m2, AX.X, ALU.add))
                step(nc.vector.scalar_tensor_tensor(out=row(2), in0=row(1), scalar=float(P // 2), in1=row(2),
                                                    op0=ALU.mult, op1=ALU.add))
                nc.vector.tensor_scalar(row(2), row(2), 1.0 / B, BN_EPS, ALU.mult,
                                        ALU.add).then_inc(var_ready, 1)
                step(nc.vector.tensor_tensor(row(1), row(0), bias, ALU.add))
                step(nc.vector.tensor_tensor(row(1), bias, row(1), ALU.subtract))
                dve.wait_ge(rstd_ready, 1)
                step(nc.vector.tensor_tensor(row(4), row(3), gain, ALU.mult))
                step(nc.vector.tensor_tensor(row(1), row(1), row(4), ALU.mult))
                return nc.vector.tensor_tensor(row(5), row(1), shift, ALU.add)

            step(batch_norm(stats1[:], M1, 0, var1_ready, rstd1_ready, b1v, g1v, be1v))
            nc.vector.tensor_copy(bn[:, 1, 0:1], bn[:, 5, 0:1]).then_inc(affine1_ready, 1)
            for m in range(0, M1, 2):
                nc.vector.tensor_scalar(y1[:, m, :], y1[:, m, :], bn[:, 4, m:m + 1], bn[:, 5, m:m + 1],
                                        ALU.mult, ALU.add).then_inc(z1_by_dve, 1)

            def dice1_measure(t):
                dve.wait_ge(z1_turned, t + 1)
                for h in range(2):
                    last = nc.vector.bn_stats(dice_stats[:, t, 6 * h:6 * h + 6], bank[z1_bank[t % 2][h]][:])
                step(last)
                step(nc.vector.bn_aggr(dice_mv[:, t, :], dice_stats[:, t, :]))
                nc.vector.tensor_scalar(dice_var[:, t:t + 1], dice_mv[:, t, 1:2], float(F1),
                                        F1 * DICE_EPS, ALU.mult, ALU.add).then_inc(dice_var_ready, 1)
                dve.wait_ge(dice_r_ready, t + 1)
                nc.vector.scalar_tensor_tensor(out=dice_nb[:, t:t + 1], in0=dice_mv[:, t, 0:1], scalar=-1.0,
                                               in1=dice_r[:, t:t + 1], op0=ALU.mult,
                                               op1=ALU.mult).then_inc(dice_nb_ready, 1)

            def dice1_apply(t):
                dve.wait_ge(sig1_ready, t + 1)
                if t >= 2:
                    dve.wait_ge(x2_turned, t - 1)
                step(nc.vector.tensor_scalar(sig1[:, t % 2, :], sig1[:, t % 2, :], one_minus[:, 0:1], alpha1,
                                             ALU.mult, ALU.add))
                for h in range(2):
                    last = nc.vector.tensor_tensor(x2[:, t % 2, h * 512:(h + 1) * 512],
                                                   sig1[:, t % 2, h * 512:(h + 1) * 512],
                                                   bank[z1_bank[t % 2][h]][:], ALU.mult)
                last.then_inc(x2_ready, 1)

            def x2_copy(t):
                dve.wait_ge(x2_turned, t + 1)
                nc.vector.tensor_copy(x2T[:, t, HALF:M1, :],
                                      bank[x2_bank[1]][:].rearrange("p (k b) -> p k b", b=P)).then_inc(x2T_by_dve, 1)

            def measure2(t):
                dve.wait_ge(y2_copied, t + 1)
                for m in range(M2):
                    last = nc.vector.bn_stats(stats2[:, m, t, :], y2[:, m, t * P:(t + 1) * P])
                last.then_inc(y2_measured, 1)

            dice1_measure(0)
            dice1_measure(1)
            for t in range(T):
                dice1_apply(t)
                x2_copy(t)
                if t >= 1:
                    measure2(t - 1)
                if t + 2 < T:
                    dice1_measure(t + 2)
            measure2(T - 1)
            dve.wait_ge(y2_measured, T)
            step(batch_norm(stats2[:], M2, 6, var2_ready, rstd2_ready, b2v, g2v, be2v))
            for m in range(M2):
                nc.vector.tensor_scalar(y2[:, m, :], y2[:, m, :], bn[:, 10, m:m + 1], bn[:, 11, m:m + 1],
                                        ALU.mult, ALU.add).then_inc(z2_ready, 1)
            for t in range(T):
                dve.wait_ge(z2_turned, t + 1)
                last = nc.vector.bn_stats(dice2_stats[:, t, :], z2_bank[t][:])
            step(last)
            for t in range(T):
                last = nc.vector.bn_aggr(dice2_mv[:, t, :], dice2_stats[:, t, :])
            step(last)
            nc.vector.tensor_scalar(dice2_var[:], dice2_mv[:, :, 1], float(F2), F2 * DICE_EPS,
                                    ALU.mult, ALU.add).then_inc(dice2_var_ready, 1)
            dve.wait_ge(w3_loaded, 16)
            nc.vector.tensor_tensor_reduce(zw[:, 0, :], z2_bank[0][:], w3[:], 1.0, 0.0, ALU.mult, ALU.add,
                                           plain[:, 0:1]).then_inc(zw_ready, 1)
            dve.wait_ge(dice2_r_ready, 1)
            nc.vector.scalar_tensor_tensor(out=dice2_nb[:], in0=dice2_mv[:, :, 0], scalar=-1.0, in1=dice2_r[:],
                                           op0=ALU.mult, op1=ALU.mult).then_inc(dice2_nb_ready, 1)
            for t in range(1, T):
                nc.vector.tensor_tensor_reduce(zw[:, t, :], z2_bank[t][:], w3[:], 1.0, 0.0, ALU.mult,
                                               ALU.add, plain[:, t:t + 1]).then_inc(zw_ready, 1)
            dve.wait_ge(zw_ready, T)
            for t in range(T):
                dve.wait_ge(sig2_ready, t + 1)
                last = nc.vector.tensor_tensor_reduce(trash[:, t, :], sig2[:, t, :], zw[:, t, :], 1.0, 0.0, ALU.mult,
                                                      ALU.add, gated[:, t:t + 1])
            step(last)
            step(nc.vector.tensor_scalar(gated[:], gated[:], one_minus[:, 1:2], bias3, ALU.mult, ALU.add))
            nc.vector.scalar_tensor_tensor(out=result[:], in0=plain[:], scalar=alpha2, in1=gated[:],
                                           op0=ALU.mult, op1=ALU.add).then_inc(result_ready, 1)

        @block.scalar
        def _(act):
            act.wait_ge(embs_turned, 1)
            nc.scalar.copy(xT[:, USER, :], turn_users[:]).then_inc(embs_copied, 1)
            act.wait_ge(embs_turned, 2)
            nc.scalar.copy(xT[:, ITEMS, :], turn_items[:]).then_inc(embs_copied, 1)
            act.wait_ge(needed_ready, 1)

            def y1_copy(t):
                act.wait_ge(y1_summed, t + 1)
                for h in range(2):
                    last = nc.scalar.copy(y1[:, h * HALF:(h + 1) * HALF, t * P:(t + 1) * P],
                                          y1_bank[t % 2][h][:].rearrange("p (m b) -> p m b", b=P))
                last.then_inc(y1_copied, 1)

            for t in range(T):
                par = t % 2
                need = act.value_load(needed[t:t + 1, 0:1], min_val=0, max_val=H)
                if t:
                    act.wait_ge(his_summed, t)
                act.wait_ge(last_scored, t + 1)
                nc.scalar.mul(last_diag[:], ident[:], last_score[:, t:t + 1]).then_inc(last_diag_ready, 1)
                if t:
                    y1_copy(t - 1)

                def quarter(i, q):
                    act.wait_ge(scored[t], QUARTERS * i + q + 1)
                    for s in range(q * QUARTER, (q + 1) * QUARTER):
                        last = nc.scalar.mul(diag[:, par, s, :], ident[:], score[:, t, s:s + 1])
                    last.then_inc(diag_ready[t], 1)

                with act.Fori(0, LOOPS) as i:
                    for q in range(QUARTERS):
                        with act.If(need > RING * i + QUARTER * q):
                            quarter(i, q)
                act.wait_ge(his_summed, t + 1)
                nc.scalar.copy(xT[:, HIS, t * P:(t + 1) * P], his_bank[par][:, 0:P]).then_inc(his_copied, 1)

            y1_copy(T - 1)
            act.wait_ge(affine1_ready, 1)
            act.wait_ge(y1_copied, T)
            for m in range(1, M1, 2):
                nc.scalar.activation(y1[:, m, :], y1[:, m, :], ACT.Identity, bias=bn[:, 5, m:m + 1],
                                     scale=bn[:, 4, m:m + 1]).then_inc(z1_by_act, 1)

            def dice1_sigmoid(t):
                act.wait_ge(dice_nb_ready, t + 1)
                for h in range(2):
                    last = nc.scalar.activation(sig1[:, t % 2, h * 512:(h + 1) * 512], bank[z1_bank[t % 2][h]][:],
                                                ACT.Sigmoid, bias=dice_nb[:, t:t + 1], scale=dice_r[:, t:t + 1])
                last.then_inc(sig1_ready, 1)

            def x2_copy(t):
                act.wait_ge(x2_turned_low, t + 1)
                nc.scalar.copy(x2T[:, t, 0:HALF, :],
                               bank[x2_bank[0]][:].rearrange("p (k b) -> p k b", b=P)).then_inc(x2T_by_act, 1)

            def y2_copy(t):
                act.wait_ge(y2_summed, t + 1)
                nc.scalar.copy(y2[:, :, t * P:(t + 1) * P],
                               y2_bank[t % 2][:].rearrange("p (m b) -> p m b", b=P)).then_inc(y2_copied, 1)

            dice1_sigmoid(0)
            dice1_sigmoid(1)
            for t in range(T):
                x2_copy(t)
                if t >= 1:
                    y2_copy(t - 1)
                if t + 2 < T:
                    dice1_sigmoid(t + 2)
            y2_copy(T - 1)
            act.wait_ge(dice2_nb_ready, 1)
            for t in range(T):
                act.wait_ge(zw_ready, t + 1)
                nc.scalar.activation(sig2[:, t, :], z2_bank[t][:], ACT.Sigmoid, bias=dice2_nb[:, t:t + 1],
                                     scale=dice2_r[:, t:t + 1]).then_inc(sig2_ready, 1)

        @block.tensor
        def _(pe):
            pe.wait_ge(ident_set, 1)
            pe.wait_ge(used_counted, 1)
            pe.transpose(bank[0][0:T, 0:P], n_used[:], ident[:]).then_inc(counts_turned, 1)
            pe.wait_ge(vectors_loaded, 16 * 6)
            pe.transpose(bank[1][:, 0:VEC], vec_rows[:], ident[0:VEC, 0:VEC]).then_inc(vectors_turned, 1)
            for t in range(T):
                pe.wait_ge(user_landed[t], 16)
                last = pe.transpose(turn_users[:, t * P:(t + 1) * P], user_emb[:, t, :], ident[:])
            last.then_inc(embs_turned, 1)
            for t in range(T):
                pe.wait_ge(item_landed[t], 16)
                last = pe.transpose(turn_items[:, t * P:(t + 1) * P], item_emb[:, t, :], ident[:])
            last.then_inc(embs_turned, 1)
            pe.wait_ge(needed_ready, 1)
            pe.wait_ge(vec_ready, 1)
            pe.wait_ge(embs_copied, 2)
            pe.wait_ge(w1_loaded, 16)

            def layer1(t, ks):
                for h in range(2):
                    for k in ks:
                        for j in range(HALF):
                            m = h * HALF + j
                            last = pe.matmul(y1_bank[t % 2][h][:, j * P:(j + 1) * P], w1[:, k, m * P:(m + 1) * P],
                                             xT[:, k, t * P:(t + 1) * P], start=(k == ITEMS and j == 0),
                                             stop=(k == HIS), skip_group_check=True)
                return last

            for t in range(T):
                par = t % 2
                need = pe.value_load(needed[t:t + 1, 0:1], min_val=0, max_val=H)
                if t >= 2:
                    pe.wait_ge(his_copied, t - 1)
                pe.matmul(his_bank[par][:, 0:P], ident[:], zeros[:], start=True, stop=False,
                          skip_group_check=True).then_inc(ring_free[t], QUARTERS)
                if t:
                    pe.wait_ge(his_copied, t)
                    layer1(t - 1, (HIS,)).then_inc(y1_summed, 1)
                if t >= 2:
                    pe.wait_ge(y1_copied, t - 1)
                layer1(t, (ITEMS, USER))

                def quarter(i, q):
                    pe.wait_ge(diag_ready[t], QUARTERS * i + q + 1)
                    for s in range(q * QUARTER, (q + 1) * QUARTER):
                        last = pe.matmul(his_bank[par][:, 0:P], ring[:, par, s, :], diag[:, par, s, :],
                                         start=False, stop=False, skip_group_check=True)
                    last.then_inc(ring_free[t], 1)

                with pe.Fori(0, LOOPS) as i:
                    for q in range(QUARTERS):
                        with pe.If(need > RING * i + QUARTER * q):
                            quarter(i, q)
                pe.wait_ge(last_diag_ready, t + 1)
                pe.matmul(his_bank[par][:, 0:P], last_row[:], last_diag[:], start=False, stop=True,
                          skip_group_check=True).then_inc(his_summed, 1)
            pe.wait_ge(his_copied, T)
            layer1(T - 1, (HIS,)).then_inc(y1_summed, 1)

            def turn_z1(t):
                if t >= 2:
                    pe.wait_ge(x2_ready, t - 1)
                for m in range(M1):
                    if t == 0:
                        pe.wait_ge(z1_by_act if m % 2 else z1_by_dve, m // 2 + 1)
                    last = pe.transpose(bank[z1_bank[t % 2][m // HALF]][:, (m % HALF) * P:(m % HALF + 1) * P],
                                        y1[:, m, t * P:(t + 1) * P], ident[:])
                last.then_inc(z1_turned, 1)

            def turn_x2(t):
                pe.wait_ge(x2_ready, t + 1)
                if t:
                    pe.wait_ge(x2T_by_act, t)
                    pe.wait_ge(x2T_by_dve, t)
                for k in range(M1):
                    last = pe.transpose(bank[x2_bank[k // HALF]][:, (k % HALF) * P:(k % HALF + 1) * P],
                                        x2[:, t % 2, k * P:(k + 1) * P], ident[:])
                    if k == HALF - 1:
                        last.then_inc(x2_turned_low, 1)
                last.then_inc(x2_turned, 1)

            def layer2(t):
                pe.wait_ge(x2T_by_act, t + 1)
                pe.wait_ge(x2T_by_dve, t + 1)
                if t >= 2:
                    pe.wait_ge(y2_copied, t - 1)
                for m in range(M2):
                    for k in range(M1):
                        last = pe.matmul(y2_bank[t % 2][:, m * P:(m + 1) * P], w2[:, k, m * P:(m + 1) * P],
                                         x2T[:, t, k, :], start=(k == 0), stop=(k == M1 - 1),
                                         skip_group_check=True)
                last.then_inc(y2_summed, 1)

            turn_z1(0)
            turn_z1(1)
            pe.wait_ge(w2_loaded, 16)
            for t in range(T):
                turn_x2(t)
                if t + 2 < T:
                    turn_z1(t + 2)
                layer2(t)
            for t in range(T):
                for m in range(M2):
                    if t == 0:
                        pe.wait_ge(z2_ready, m + 1)
                    last = pe.transpose(z2_bank[t][:, m * P:(m + 1) * P], y2[:, m, t * P:(t + 1) * P], ident[:])
                last.then_inc(z2_turned, 1)


_INS = ['r_items', 'r_users', 'r_history_users', 'L0_rec_item_table', 'L0_rec_user_table', 'L0_rec_W1',
        'L0_rec_b1', 'L0_rec_g1', 'L0_rec_be1', 'L0_rec_a1', 'L0_rec_W2', 'L0_rec_b2', 'L0_rec_g2',
        'L0_rec_be2', 'L0_rec_a2', 'L0_rec_W3', 'L0_rec_b3']


def kernel(**inputs):
    import numpy as np
    import concourse.bacc as bacc
    from concourse.bass_utils import run_bass_kernel_spmd

    nc = bacc.Bacc("TRN2", target_bir_lowering=False, num_devices=1)
    arrays, args = {}, []
    for name in _INS:
        a = np.ascontiguousarray(inputs[name])
        arrays[f"in_{name}"] = a
        args.append(nc.dram_tensor(f"in_{name}", a.shape, mybir.dt.from_np(a.dtype), kind="ExternalInput").ap())
    batch = inputs['r_items'].shape[0]
    args.append(nc.dram_tensor("out", (batch, 1), F32, kind="ExternalOutput").ap())
    recommender_kernel(nc, *args)
    r = run_bass_kernel_spmd(nc, [arrays], core_ids=[0])
    return r.results[0]["out"]
```

```python
from contextlib import ExitStack

import concourse.bass as bass
from concourse import mybir

F32 = mybir.dt.float32
I32 = mybir.dt.int32
ALU = mybir.AluOpType
ACT = mybir.ActivationFunctionType
AX = mybir.AxisListType

P = 128
QUARTER = 2
RING = 16
GROUP = 8
QUARTERS = RING // QUARTER
USUAL = 3
DICE_EPS = 1e-3
BN_EPS = 1e-5


def recommender_kernel(nc, items, users, history, item_table, user_table, W1, b1, g1, be1, a1,
                       W2, b2, g2, be2, a2, W3, b3, out):
    B, H = history.shape
    n_item, D = item_table.shape
    n_user = user_table.shape[0]
    d_in, F1 = W1.shape
    F2 = W2.shape[1]
    T = B // P
    M1, M2 = F1 // P, F2 // P
    KIN = d_in // P
    ITEMS, HIS, USER = range(KIN)
    HALF = M1 // 2
    PAD = -(-H // GROUP) * GROUP
    LOOPS = -(-H // RING)
    VEC = 3 * M1 + 3 * M2
    assert D == P and KIN == 3 and HALF * P == 512 and F2 == 512 and T == 4

    with ExitStack() as ctx:
        def sb(name, shape, dt=F32):
            return ctx.enter_context(nc.sbuf_tensor(name, shape, dt))

        def sem(name):
            return ctx.enter_context(nc.semaphore(name))

        bank = [ctx.enter_context(nc.psum_tensor(f"bank{i}", [P, 512], F32)) for i in range(8)]

        raw_users, raw_items = sb("raw_users", [P, T], I32), sb("raw_items", [P, T], I32)
        raw_history = sb("raw_history", [P, T, H], I32)
        wrap_u, wrap_i = sb("wrap_u", [P, T]), sb("wrap_i", [P, T])
        wrap_h = sb("wrap_h", [P, T, H])
        user_rows, item_rows = sb("user_rows", [P, T], I32), sb("item_rows", [P, T], I32)
        keys = sb("keys", [P, T, PAD])
        used = sb("used", [P, T, PAD])
        n_used, n_last = sb("n_used", [P, T]), sb("n_last", [P, T])
        needed = sb("needed", [T, 1], I32)
        top = sb("top", [P, T, 2, GROUP])
        slot_mask = sb("slot_mask", [P, T, 2, GROUP])
        slot_row = sb("slot_row", [P, T, 2, GROUP], I32)
        user_emb, item_emb = sb("user_emb", [P, T, D]), sb("item_emb", [P, T, D])
        ring = sb("ring", [P, 2, RING, D])
        last_row = sb("last_row", [P, D])
        product = sb("product", [P, 2, RING, D])
        last_product = sb("last_product", [P, T, D])
        score = sb("score", [P, T, RING])
        last_score = sb("last_score", [P, T])
        diag = sb("diag", [P, 2, RING, P])
        last_diag = sb("last_diag", [P, P])
        ident, zeros = sb("ident", [P, P]), sb("zeros", [P, P])
        minus_half = sb("minus_half", [P, M1])
        w1, w2 = sb("w1", [P, KIN, F1]), sb("w2", [P, M1, F2])
        w3 = sb("w3", [P, F2])
        vec_rows, vec = sb("vec_rows", [VEC, P]), sb("vec", [P, VEC])
        scalars, one_minus = sb("scalars", [P, 3]), sb("one_minus", [P, 2])
        xT = sb("xT", [P, KIN, B])
        y1 = sb("y1", [P, M1, B])
        stats1 = sb("stats1", [P, M1, T, 6])
        sig1 = sb("sig1", [P, 2, F1])
        x2 = sb("x2", [P, 2, F1])
        x2T = sb("x2T", [P, T, M1, P])
        y2 = sb("y2", [P, M2, B])
        stats2 = sb("stats2", [P, M2, T, 6])
        sig2, zw = sb("sig2", [P, T, F2]), sb("zw", [P, T, F2])
        bn = sb("bn", [P, 12, M1])
        bn_mv = sb("bn_mv", [P, M1, 2])
        dice_stats = sb("dice_stats", [P, T, 12])
        dice_mv, dice_var = sb("dice_mv", [P, T, 2]), sb("dice_var", [P, T])
        dice_r, dice_nb = sb("dice_r", [P, T]), sb("dice_nb", [P, T])
        dice2_stats, dice2_mv = sb("dice2_stats", [P, T, 6]), sb("dice2_mv", [P, T, 2])
        dice2_var, dice2_r = sb("dice2_var", [P, T]), sb("dice2_r", [P, T])
        dice2_nb = sb("dice2_nb", [P, T])
        trash = sb("trash", [P, T, F2])
        plain, gated = sb("plain", [P, T]), sb("gated", [P, T])
        result = sb("result", [P, T])

        b1v, g1v, be1v = (vec[:, i * M1:(i + 1) * M1] for i in range(3))
        b2v, g2v, be2v = (vec[:, 3 * M1 + i * M2:3 * M1 + (i + 1) * M2] for i in range(3))
        alpha1, alpha2, bias3 = (scalars[:, i:i + 1] for i in range(3))

        users_loaded, items_loaded = sem("users_loaded"), sem("items_loaded")
        history_loaded, last_row_loaded = sem("history_loaded"), sem("last_row_loaded")
        vectors_loaded, w1_loaded, w2_loaded = sem("vectors_loaded"), sem("w1_loaded"), sem("w2_loaded")
        w3_loaded, scalars_loaded = sem("w3_loaded"), sem("scalars_loaded")
        zeros_set, ident_set, halves_set = sem("zeros_set"), sem("ident_set"), sem("halves_set")
        dve_step = sem("dve_step")
        user_rows_ready, item_rows_ready = sem("user_rows_ready"), sem("item_rows_ready")
        used_counted, counts_turned = sem("used_counted"), sem("counts_turned")
        needed_ready = sem("needed_ready")
        user_landed = [sem(f"user_landed{t}") for t in range(T)]
        item_landed = [sem(f"item_landed{t}") for t in range(T)]
        embs_turned, embs_copied = sem("embs_turned"), sem("embs_copied")
        vectors_turned, vec_ready = sem("vectors_turned"), sem("vec_ready")
        top_found = [sem(f"top_found{t}") for t in range(T)]
        keys_cut = [sem(f"keys_cut{t}") for t in range(T)]
        mask_ready = [sem(f"mask_ready{t}") for t in range(T)]
        rows_ready = [sem(f"rows_ready{t}") for t in range(T)]
        landed = [[sem(f"landed{t}_{q}") for q in range(QUARTERS)] for t in range(T)]
        scored = [sem(f"scored{t}") for t in range(T)]
        last_scored = sem("last_scored")
        diag_ready = [sem(f"diag_ready{t}") for t in range(T)]
        last_diag_ready = sem("last_diag_ready")
        ring_free = [sem(f"ring_free{t}") for t in range(T)]
        his_summed, his_copied = sem("his_summed"), sem("his_copied")
        gathering, sorting = sem("gathering"), sem("sorting")
        y1_summed, y1_copied = sem("y1_summed"), sem("y1_copied")
        var1_ready, rstd1_ready, affine1_ready = sem("var1_ready"), sem("rstd1_ready"), sem("affine1_ready")
        z1_by_act, z1_by_dve, z1_by_pool = sem("z1_by_act"), sem("z1_by_dve"), sem("z1_by_pool")
        y1_measured = sem("y1_measured")
        z1_turned, dice_var_ready, dice_r_ready = sem("z1_turned"), sem("dice_var_ready"), sem("dice_r_ready")
        dice_nb_ready, sig1_ready, x2_ready = sem("dice_nb_ready"), sem("sig1_ready"), sem("x2_ready")
        x2_turned_low, x2_turned = sem("x2_turned_low"), sem("x2_turned")
        x2T_by_act, x2T_by_dve = sem("x2T_by_act"), sem("x2T_by_dve")
        y2_summed, y2_copied, y2_measured = sem("y2_summed"), sem("y2_copied"), sem("y2_measured")
        var2_ready, rstd2_ready, z2_ready = sem("var2_ready"), sem("rstd2_ready"), sem("z2_ready")
        z2_turned, dice2_var_ready, dice2_r_ready = sem("z2_turned"), sem("dice2_var_ready"), sem("dice2_r_ready")
        dice2_nb_ready, sig2_ready, zw_ready = sem("dice2_nb_ready"), sem("sig2_ready"), sem("zw_ready")
        result_ready, stored = sem("result_ready"), sem("stored")

        his_bank = [bank[0], bank[1]]
        y1_bank = [(bank[2], bank[3]), (bank[4], bank[5])]
        turn_items, turn_users = bank[6], bank[7]
        z1_bank = [(0, 1), (2, 3)]
        x2_bank = (4, 5)
        y2_bank = [bank[6], bank[7]]
        z2_bank = [bank[0], bank[1], bank[2], bank[3]]

        block = ctx.enter_context(nc.Block())

        @block.sync
        def _(sp):
            sp.dma_start(raw_users[:], users.rearrange("(p t) -> p t", t=T)).then_inc(users_loaded, 16)
            sp.dma_start(raw_history[:], history.rearrange("(p t) h -> p t h", t=T)).then_inc(history_loaded, 16)
            sp.dma_start(raw_items[:], items.rearrange("(p t) -> p t", t=T)).then_inc(items_loaded, 16)
            sp.dma_start(last_row[:], user_table[n_user - 1, :].partition_broadcast(P)).then_inc(last_row_loaded, 16)
            row = 0
            for v in (b1, g1, be1, b2, g2, be2):
                n = v.shape[0] // P
                sp.dma_start(vec_rows[row:row + n, :], v.rearrange("(m p) -> m p", p=P)).then_inc(vectors_loaded, 16)
                row += n
            sp.dma_start(w3[:], W3.rearrange("f o -> (f o)").partition_broadcast(P)).then_inc(w3_loaded, 16)
            for i, v in enumerate((a1, a2, b3)):
                sp.dma_start(scalars[:, i:i + 1], v.partition_broadcast(P)).then_inc(scalars_loaded, 16)
            for t in range(T):
                sp.wait_ge(user_landed[t], 16)
            sp.dma_start(w1[:], W1.rearrange("(k p) f -> p k f", p=P)).then_inc(w1_loaded, 16)
            sp.wait_ge(w1_loaded, 16)
            sp.dma_start(w2[:], W2.rearrange("(k p) f -> p k f", p=P)).then_inc(w2_loaded, 16)
            sp.wait_ge(result_ready, 1)
            sp.dma_start(out.rearrange("(p t) o -> p (t o)", t=T), result[:]).then_inc(stored, 16)
            sp.wait_ge(stored, 16)

        @block.gpsimd
        def _(pool):
            pool.wait_ge(zeros_set, 1)
            nc.gpsimd.affine_select(out=ident[:], in_=zeros[:], compare_op=ALU.not_equal, fill=1.0, base=0,
                                    pattern=[[-1, P]], channel_multiplier=1).then_inc(ident_set, 1)

            def gather(dst, table, rows):
                return nc.gpsimd.indirect_dma_start(dst, None, table[:, :],
                                                    bass.IndirectOffsetOnAxis(ap=rows, axis=0))

            pool.wait_ge(user_rows_ready, 1)
            for t in range(T):
                gather(user_emb[:, t, :], user_table, user_rows[:, t:t + 1]).then_inc(user_landed[t], 16)
            pool.wait_ge(item_rows_ready, 1)
            for t in range(T):
                gather(item_emb[:, t, :], item_table, item_rows[:, t:t + 1]).then_inc(item_landed[t], 16)

            pool.wait_ge(needed_ready, 1)
            needs = [pool.value_load(needed[t:t + 1, 0:1], min_val=0, max_val=H) for t in range(T)]
            for t in range(T):
                par, need = t % 2, needs[t]

                def quarter(i, q):
                    group = q * QUARTER // GROUP
                    pool.wait_ge(rows_ready[t], 2 * i + group + 1)
                    pool.wait_ge(ring_free[t], QUARTERS * i + q + 1)
                    pool.sem_inc(gathering, 1)
                    for s in range(q * QUARTER, (q + 1) * QUARTER):
                        gather(ring[:, par, s, :], user_table,
                               slot_row[:, t, group, s % GROUP:s % GROUP + 1]).then_inc(landed[t][q], 16)

                def iteration(i, q=0):
                    with pool.If(need > RING * i + QUARTER * q):
                        quarter(i, q)
                        if q + 1 < QUARTERS:
                            iteration(i, q + 1)

                with pool.Fori(0, USUAL) as i:
                    iteration(i)
                with pool.If(need > RING * USUAL):
                    with pool.Fori(USUAL, LOOPS) as i:
                        iteration(i)

            def rsqrt(dst, src, n):
                return nc.gpsimd.tensor_tensor(dst, src, minus_half[:, 0:n], ALU.pow)

            pool.wait_ge(halves_set, 1)
            pool.wait_ge(var1_ready, 1)
            rsqrt(bn[:, 3, :], bn[:, 2, :], M1).then_inc(rstd1_ready, 1)
            pool.wait_ge(affine1_ready, 1)
            pool.wait_ge(y1_copied, T)

            def normalize1(m):
                nc.gpsimd.tensor_scalar(y1[:, m, 2 * P:B], y1[:, m, 2 * P:B], bn[:, 4, m:m + 1],
                                        bn[:, 5, m:m + 1], ALU.mult, ALU.add).then_inc(z1_by_pool, 1)

            for m in range(M1 // 2):
                normalize1(m)
            for t in range(T):
                pool.wait_ge(dice_var_ready, t + 1)
                rsqrt(dice_r[:, t:t + 1], dice_var[:, t:t + 1], 1).then_inc(dice_r_ready, 1)
                if t == 0:
                    for m in range(M1 // 2, M1):
                        normalize1(m)
            pool.wait_ge(var2_ready, 1)
            rsqrt(bn[:, 9, 0:M2], bn[:, 8, 0:M2], M2).then_inc(rstd2_ready, 1)
            for t in range(T):
                pool.wait_ge(dice2_var_ready, t + 1)
                rsqrt(dice2_r[:, t:t + 1], dice2_var[:, t:t + 1], 1).then_inc(dice2_r_ready, 1)

        @block.vector
        def _(dve):
            steps = [0]

            def step(ins):
                steps[0] += 1
                ins.then_inc(dve_step, 1)
                dve.wait_ge(dve_step, steps[0])

            nc.vector.memset(zeros[:], 0.0).then_inc(zeros_set, 1)
            nc.vector.memset(minus_half[:], -0.5).then_inc(halves_set, 1)
            step(nc.vector.memset(keys[:], 0.0))

            def clamp(raw, wrap, n):
                step(nc.vector.tensor_scalar(wrap, raw, 0.0, float(n), ALU.is_lt, ALU.mult))
                step(nc.vector.tensor_tensor(wrap, raw, wrap, ALU.add))
                step(nc.vector.tensor_scalar(wrap, wrap, 0.0, -1.0, ALU.max, ALU.mult))

            dve.wait_ge(users_loaded, 16)
            clamp(raw_users[:], wrap_u[:], n_user)
            step(nc.vector.tensor_scalar(wrap_u[:], wrap_u[:], float(n_user - 1), 0.0, ALU.add, ALU.max))
            nc.vector.tensor_scalar(user_rows[:], wrap_u[:], -1.0, float(n_user - 1),
                                    ALU.mult, ALU.add).then_inc(user_rows_ready, 1)
            dve.wait_ge(items_loaded, 16)
            clamp(raw_items[:], wrap_i[:], n_item)
            step(nc.vector.tensor_scalar(wrap_i[:], wrap_i[:], float(n_item - 1), 0.0, ALU.add, ALU.max))
            nc.vector.tensor_scalar(item_rows[:], wrap_i[:], -1.0, float(n_item - 1),
                                    ALU.mult, ALU.add).then_inc(item_rows_ready, 1)
            dve.wait_ge(history_loaded, 16)
            clamp(raw_history[:], wrap_h[:], n_user)
            step(nc.vector.tensor_scalar(keys[:, :, 0:H], wrap_h[:], float(n_user - 1), 0.0, ALU.add, ALU.max))
            step(nc.vector.tensor_scalar(used[:], keys[:], 1.0, None, ALU.min))
            nc.vector.tensor_reduce(n_used[:], used[:], AX.X, ALU.add).then_inc(used_counted, 1)

            def sort(t, group, n):
                par = t % 2
                dve.wait_ge(keys_cut[t], n)
                dve.sem_inc(sorting, 1)
                nc.vector.max(top[:, t, group, :], keys[:, t, :]).then_inc(top_found[t], 1)
                dve.wait_ge(top_found[t], n + 1)
                nc.vector.tensor_scalar(slot_row[:, t, group, :], top[:, t, group, :], -1.0,
                                        float(n_user - 1), ALU.mult, ALU.add).then_inc(rows_ready[t], 1)
                nc.vector.tensor_scalar(slot_mask[:, t, group, :], top[:, t, group, :], 1.0, None,
                                        ALU.min).then_inc(mask_ready[t], 1)
                nc.vector.match_replace(keys[:, t, :], top[:, t, group, :], keys[:, t, :],
                                        0.0).then_inc(keys_cut[t], 1)

            def first_sorts(t):
                par = t % 2
                nc.vector.max(top[:, t, 0, :], keys[:, t, :]).then_inc(top_found[t], 1)
                dve.wait_ge(top_found[t], 1)
                nc.vector.tensor_scalar(slot_row[:, t, 0, :], top[:, t, 0, :], -1.0,
                                        float(n_user - 1), ALU.mult, ALU.add).then_inc(rows_ready[t], 1)
                nc.vector.tensor_scalar(slot_mask[:, t, 0, :], top[:, t, 0, :], 1.0, None,
                                        ALU.min).then_inc(mask_ready[t], 1)
                nc.vector.match_replace(keys[:, t, :], top[:, t, 0, :], keys[:, t, :],
                                        0.0).then_inc(keys_cut[t], 1)
                sort(t, 1, 1)

            dve.wait_ge(counts_turned, 1)
            nc.vector.tensor_reduce(needed[:], bank[2][0:T, 0:P], AX.X, ALU.max).then_inc(needed_ready, 1)
            step(nc.vector.tensor_scalar(n_last[:], n_used[:], -1.0, float(H), ALU.mult, ALU.add))
            first_sorts(0)
            dve.wait_ge(scalars_loaded, 48)
            nc.vector.tensor_scalar(one_minus[:], scalars[:, 0:2], -1.0, 1.0, ALU.mult, ALU.add)
            dve.wait_ge(vectors_turned, 1)
            nc.vector.tensor_copy(vec[:], bank[3][:, 0:VEC]).then_inc(vec_ready, 1)
            dve.wait_ge(last_row_loaded, 16)
            dve.wait_ge(needed_ready, 1)

            def measure1(t):
                dve.wait_ge(y1_copied, t + 1)
                for m in range(M1):
                    last = nc.vector.bn_stats(stats1[:, m, t, :], y1[:, m, t * P:(t + 1) * P])
                return last

            needs = [dve.value_load(needed[t:t + 1, 0:1], min_val=0, max_val=H) for t in range(T)]
            for t in range(T):
                par, need = t % 2, needs[t]
                dve.wait_ge(user_landed[t], 16)
                nc.vector.tensor_tensor_reduce(last_product[:, t, :], last_row[:], user_emb[:, t, :], n_last[:, t:t + 1],
                                               0.0, ALU.mult, ALU.add,
                                               last_score[:, t:t + 1]).then_inc(last_scored, 1)
                if t + 1 < T:
                    first_sorts(t + 1)
                if t:
                    measure1(t - 1)

                def quarter(i, q):
                    group = q * QUARTER // GROUP
                    dve.wait_ge(mask_ready[t], 2 * i + group + 1)
                    dve.wait_ge(landed[t][q], 16 * QUARTER * (i + 1))
                    for s in range(q * QUARTER, (q + 1) * QUARTER):
                        last = nc.vector.tensor_tensor_reduce(
                            product[:, par, s, :], ring[:, par, s, :], user_emb[:, t, :],
                            slot_mask[:, t, group, s % GROUP:s % GROUP + 1], 0.0, ALU.mult, ALU.add,
                            score[:, t, s:s + 1])
                    last.then_inc(scored[t], 1)

                def iteration(i, q=0):
                    with dve.If(need > RING * i + QUARTER * q):
                        quarter(i, q)
                        if (q + 1) * QUARTER % GROUP == 0:
                            group = q * QUARTER // GROUP
                            with dve.If(need > RING * (i + 1) + GROUP * group):
                                sort(t, group, 2 * i + 2 + group)
                        if q + 1 < QUARTERS:
                            iteration(i, q + 1)

                with dve.Fori(0, USUAL) as i:
                    iteration(i)
                with dve.If(need > RING * USUAL):
                    with dve.Fori(USUAL, LOOPS) as i:
                        iteration(i)

            for h in range(2):
                dve.wait_ge(y1_summed, T + h)
                for j in range(HALF):
                    last = nc.vector.bn_stats(stats1[:, h * HALF + j, T - 1, :],
                                              y1_bank[(T - 1) % 2][h][:, j * P:(j + 1) * P])
                last.then_inc(y1_measured, 1)
            dve.wait_ge(y1_measured, 2)

            def batch_norm(stats, M, base, var_ready, rstd_ready, bias, gain, shift):
                row = lambda n: bn[:, base + n, 0:M]
                for m in range(M):
                    last = nc.vector.bn_aggr(bn_mv[:, m, :], stats[:, m, :, :].rearrange("p t c -> p (t c)"))
                step(last)
                nc.vector.tensor_scalar(row(2), bn_mv[:, 0:M, 1], BN_EPS, None, ALU.add).then_inc(var_ready, 1)
                step(nc.vector.tensor_tensor(row(0), bn_mv[:, 0:M, 0], bias, ALU.add))
                step(nc.vector.tensor_tensor(row(1), bias, row(0), ALU.subtract))
                dve.wait_ge(rstd_ready, 1)
                step(nc.vector.tensor_tensor(row(4), row(3), gain, ALU.mult))
                step(nc.vector.tensor_tensor(row(1), row(1), row(4), ALU.mult))
                return nc.vector.tensor_tensor(row(5), row(1), shift, ALU.add)

            batch_norm(stats1[:], M1, 0, var1_ready, rstd1_ready, b1v, g1v, be1v).then_inc(affine1_ready, 1)
            dve.wait_ge(affine1_ready, 1)
            for m in range(M1):
                nc.vector.tensor_scalar(y1[:, m, 0:P], y1[:, m, 0:P], bn[:, 4, m:m + 1], bn[:, 5, m:m + 1],
                                        ALU.mult, ALU.add).then_inc(z1_by_dve, 1)

            def dice1_measure(t):
                dve.wait_ge(z1_turned, t + 1)
                for h in range(2):
                    last = nc.vector.bn_stats(dice_stats[:, t, 6 * h:6 * h + 6], bank[z1_bank[t % 2][h]][:])
                step(last)
                step(nc.vector.bn_aggr(dice_mv[:, t, :], dice_stats[:, t, :]))
                nc.vector.tensor_scalar(dice_var[:, t:t + 1], dice_mv[:, t, 1:2], float(F1),
                                        F1 * DICE_EPS, ALU.mult, ALU.add).then_inc(dice_var_ready, 1)
                dve.wait_ge(dice_r_ready, t + 1)
                nc.vector.scalar_tensor_tensor(out=dice_nb[:, t:t + 1], in0=dice_mv[:, t, 0:1], scalar=-1.0,
                                               in1=dice_r[:, t:t + 1], op0=ALU.mult,
                                               op1=ALU.mult).then_inc(dice_nb_ready, 1)

            def dice1_apply(t):
                dve.wait_ge(sig1_ready, t + 1)
                if t >= 2:
                    dve.wait_ge(x2_turned, t - 1)
                step(nc.vector.tensor_scalar(sig1[:, t % 2, :], sig1[:, t % 2, :], one_minus[:, 0:1], alpha1,
                                             ALU.mult, ALU.add))
                for h in range(2):
                    last = nc.vector.tensor_tensor(x2[:, t % 2, h * 512:(h + 1) * 512],
                                                   sig1[:, t % 2, h * 512:(h + 1) * 512],
                                                   bank[z1_bank[t % 2][h]][:], ALU.mult)
                last.then_inc(x2_ready, 1)

            def x2_copy(t):
                dve.wait_ge(x2_turned, t + 1)
                nc.vector.tensor_copy(x2T[:, t, HALF:M1, :],
                                      bank[x2_bank[1]][:].rearrange("p (k b) -> p k b", b=P)).then_inc(x2T_by_dve, 1)

            def measure2(t):
                dve.wait_ge(y2_copied, t + 1)
                for m in range(M2):
                    last = nc.vector.bn_stats(stats2[:, m, t, :], y2[:, m, t * P:(t + 1) * P])
                last.then_inc(y2_measured, 1)

            dice1_measure(0)
            dice1_measure(1)
            for t in range(T):
                dice1_apply(t)
                x2_copy(t)
                if t >= 1:
                    measure2(t - 1)
                if t + 2 < T:
                    dice1_measure(t + 2)
            dve.wait_ge(y2_summed, T)
            for m in range(M2):
                last = nc.vector.bn_stats(stats2[:, m, T - 1, :], y2_bank[(T - 1) % 2][:, m * P:(m + 1) * P])
            last.then_inc(y2_measured, 1)
            dve.wait_ge(y2_measured, T)
            step(batch_norm(stats2[:], M2, 6, var2_ready, rstd2_ready, b2v, g2v, be2v))
            dve.wait_ge(y2_copied, T)
            for m in range(M2):
                nc.vector.tensor_scalar(y2[:, m, :], y2[:, m, :], bn[:, 10, m:m + 1], bn[:, 11, m:m + 1],
                                        ALU.mult, ALU.add).then_inc(z2_ready, 1)

            def dice2_measure(t):
                dve.wait_ge(z2_turned, t + 1)
                step(nc.vector.bn_stats(dice2_stats[:, t, :], z2_bank[t][:]))
                step(nc.vector.bn_aggr(dice2_mv[:, t, :], dice2_stats[:, t, :]))
                nc.vector.tensor_scalar(dice2_var[:, t:t + 1], dice2_mv[:, t, 1:2], float(F2), F2 * DICE_EPS,
                                        ALU.mult, ALU.add).then_inc(dice2_var_ready, 1)

            def dice2_weigh(t):
                nc.vector.tensor_tensor_reduce(zw[:, t, :], z2_bank[t][:], w3[:], 1.0, 0.0, ALU.mult, ALU.add,
                                               plain[:, t:t + 1]).then_inc(zw_ready, 1)
                dve.wait_ge(dice2_r_ready, t + 1)
                nc.vector.scalar_tensor_tensor(out=dice2_nb[:, t:t + 1], in0=dice2_mv[:, t, 0:1], scalar=-1.0,
                                               in1=dice2_r[:, t:t + 1], op0=ALU.mult,
                                               op1=ALU.mult).then_inc(dice2_nb_ready, 1)

            def dice2_gate(t):
                dve.wait_ge(sig2_ready, t + 1)
                dve.wait_ge(zw_ready, t + 1)
                return nc.vector.tensor_tensor_reduce(trash[:, t, :], sig2[:, t, :], zw[:, t, :], 1.0, 0.0,
                                                      ALU.mult, ALU.add, gated[:, t:t + 1])

            dve.wait_ge(w3_loaded, 16)
            for t in range(T):
                dice2_measure(t)
                dice2_weigh(t)
                if t:
                    dice2_gate(t - 1)
            last = dice2_gate(T - 1)
            step(last)
            step(nc.vector.tensor_scalar(gated[:], gated[:], one_minus[:, 1:2], bias3, ALU.mult, ALU.add))
            nc.vector.scalar_tensor_tensor(out=result[:], in0=plain[:], scalar=alpha2, in1=gated[:],
                                           op0=ALU.mult, op1=ALU.add).then_inc(result_ready, 1)

        @block.scalar
        def _(act):
            act.wait_ge(embs_turned, 1)
            nc.scalar.copy(xT[:, USER, :], turn_users[:]).then_inc(embs_copied, 1)
            act.wait_ge(embs_turned, 2)
            nc.scalar.copy(xT[:, ITEMS, :], turn_items[:]).then_inc(embs_copied, 1)
            act.wait_ge(needed_ready, 1)

            def y1_copy(t):
                act.wait_ge(y1_summed, t + 1)
                for h in range(2):
                    if t == T - 1:
                        act.wait_ge(y1_measured, h + 1)
                    last = nc.scalar.copy(y1[:, h * HALF:(h + 1) * HALF, t * P:(t + 1) * P],
                                          y1_bank[t % 2][h][:].rearrange("p (m b) -> p m b", b=P))
                last.then_inc(y1_copied, 1)

            needs = [act.value_load(needed[t:t + 1, 0:1], min_val=0, max_val=H) for t in range(T)]
            for t in range(T):
                par, need = t % 2, needs[t]
                if t:
                    act.wait_ge(his_summed, t)
                act.wait_ge(last_scored, t + 1)
                nc.scalar.mul(last_diag[:], ident[:], last_score[:, t:t + 1]).then_inc(last_diag_ready, 1)
                if t:
                    y1_copy(t - 1)

                def quarter(i, q):
                    act.wait_ge(scored[t], QUARTERS * i + q + 1)
                    for s in range(q * QUARTER, (q + 1) * QUARTER):
                        last = nc.scalar.mul(diag[:, par, s, :], ident[:], score[:, t, s:s + 1])
                    last.then_inc(diag_ready[t], 1)

                def iteration(i, q=0):
                    with act.If(need > RING * i + QUARTER * q):
                        quarter(i, q)
                        if q + 1 < QUARTERS:
                            iteration(i, q + 1)

                with act.Fori(0, USUAL) as i:
                    iteration(i)
                with act.If(need > RING * USUAL):
                    with act.Fori(USUAL, LOOPS) as i:
                        iteration(i)
                act.wait_ge(his_summed, t + 1)
                nc.scalar.copy(xT[:, HIS, t * P:(t + 1) * P], his_bank[par][:, 0:P]).then_inc(his_copied, 1)

            y1_copy(T - 1)
            act.wait_ge(affine1_ready, 1)
            act.wait_ge(y1_copied, T)
            for m in range(M1):
                last = nc.scalar.activation(y1[:, m, P:2 * P], y1[:, m, P:2 * P], ACT.Identity,
                                            bias=bn[:, 5, m:m + 1], scale=bn[:, 4, m:m + 1])
            last.then_inc(z1_by_act, 1)

            def dice1_sigmoid(t):
                act.wait_ge(dice_nb_ready, t + 1)
                for h in range(2):
                    last = nc.scalar.activation(sig1[:, t % 2, h * 512:(h + 1) * 512], bank[z1_bank[t % 2][h]][:],
                                                ACT.Sigmoid, bias=dice_nb[:, t:t + 1], scale=dice_r[:, t:t + 1])
                last.then_inc(sig1_ready, 1)

            def x2_copy(t):
                act.wait_ge(x2_turned_low, t + 1)
                nc.scalar.copy(x2T[:, t, 0:HALF, :],
                               bank[x2_bank[0]][:].rearrange("p (k b) -> p k b", b=P)).then_inc(x2T_by_act, 1)

            def y2_copy(t):
                act.wait_ge(y2_summed, t + 1)
                if t == T - 1:
                    act.wait_ge(y2_measured, T)
                nc.scalar.copy(y2[:, :, t * P:(t + 1) * P],
                               y2_bank[t % 2][:].rearrange("p (m b) -> p m b", b=P)).then_inc(y2_copied, 1)

            dice1_sigmoid(0)
            dice1_sigmoid(1)
            for t in range(T):
                x2_copy(t)
                if t >= 1:
                    y2_copy(t - 1)
                if t + 2 < T:
                    dice1_sigmoid(t + 2)
            y2_copy(T - 1)
            for t in range(T):
                act.wait_ge(dice2_nb_ready, t + 1)
                act.wait_ge(zw_ready, t + 1)
                nc.scalar.activation(sig2[:, t, :], z2_bank[t][:], ACT.Sigmoid, bias=dice2_nb[:, t:t + 1],
                                     scale=dice2_r[:, t:t + 1]).then_inc(sig2_ready, 1)

        @block.tensor
        def _(pe):
            pe.wait_ge(ident_set, 1)

            def open_ring(t):
                pe.matmul(his_bank[t % 2][:, 0:P], ident[:], zeros[:], start=True, stop=False,
                          skip_group_check=True).then_inc(ring_free[t], QUARTERS)

            open_ring(0)
            open_ring(1)
            pe.wait_ge(used_counted, 1)
            pe.transpose(bank[2][0:T, 0:P], n_used[:], ident[:]).then_inc(counts_turned, 1)
            pe.wait_ge(vectors_loaded, 16 * 6)
            pe.transpose(bank[3][:, 0:VEC], vec_rows[:], ident[0:VEC, 0:VEC]).then_inc(vectors_turned, 1)
            for t in range(T):
                pe.wait_ge(user_landed[t], 16)
                last = pe.transpose(turn_users[:, t * P:(t + 1) * P], user_emb[:, t, :], ident[:])
            last.then_inc(embs_turned, 1)
            pe.wait_ge(needed_ready, 1)
            for t in range(T):
                pe.wait_ge(item_landed[t], 16)
                last = pe.transpose(turn_items[:, t * P:(t + 1) * P], item_emb[:, t, :], ident[:])
            last.then_inc(embs_turned, 1)
            needs = [pe.value_load(needed[t:t + 1, 0:1], min_val=0, max_val=H) for t in range(T)]
            pe.wait_ge(vec_ready, 1)
            pe.wait_ge(embs_copied, 2)
            pe.wait_ge(w1_loaded, 16)

            def layer1(t, ks, halves=(0, 1)):
                for h in halves:
                    for k in ks:
                        for j in range(HALF):
                            m = h * HALF + j
                            last = pe.matmul(y1_bank[t % 2][h][:, j * P:(j + 1) * P], w1[:, k, m * P:(m + 1) * P],
                                             xT[:, k, t * P:(t + 1) * P], start=(k == ITEMS and j == 0),
                                             stop=(k == HIS), skip_group_check=True)
                return last

            for t in range(T):
                par, need = t % 2, needs[t]
                if t:
                    pe.wait_ge(his_copied, t)
                    if t + 1 < T:
                        open_ring(t + 1)
                    layer1(t - 1, (HIS,)).then_inc(y1_summed, 1)
                if t >= 2:
                    pe.wait_ge(y1_copied, t - 1)
                layer1(t, (ITEMS, USER))

                def quarter(i, q):
                    pe.wait_ge(diag_ready[t], QUARTERS * i + q + 1)
                    for s in range(q * QUARTER, (q + 1) * QUARTER):
                        last = pe.matmul(his_bank[par][:, 0:P], ring[:, par, s, :], diag[:, par, s, :],
                                         start=False, stop=False, skip_group_check=True)
                    last.then_inc(ring_free[t], 1)

                def iteration(i, q=0):
                    with pe.If(need > RING * i + QUARTER * q):
                        quarter(i, q)
                        if q + 1 < QUARTERS:
                            iteration(i, q + 1)

                with pe.Fori(0, USUAL) as i:
                    iteration(i)
                with pe.If(need > RING * USUAL):
                    with pe.Fori(USUAL, LOOPS) as i:
                        iteration(i)
                pe.wait_ge(last_diag_ready, t + 1)
                pe.matmul(his_bank[par][:, 0:P], last_row[:], last_diag[:], start=False, stop=True,
                          skip_group_check=True).then_inc(his_summed, 1)
            pe.wait_ge(his_copied, T)
            for h in range(2):
                layer1(T - 1, (HIS,), (h,)).then_inc(y1_summed, 1)

            def turn_z1(t):
                if t == 1:
                    pe.wait_ge(z1_by_act, 1)
                if t >= 2:
                    pe.wait_ge(x2_ready, t - 1)
                for m in range(M1):
                    if t == 0:
                        pe.wait_ge(z1_by_dve, m + 1)
                    elif t == 2:
                        pe.wait_ge(z1_by_pool, m + 1)
                    last = pe.transpose(bank[z1_bank[t % 2][m // HALF]][:, (m % HALF) * P:(m % HALF + 1) * P],
                                        y1[:, m, t * P:(t + 1) * P], ident[:])
                last.then_inc(z1_turned, 1)

            def turn_x2(t):
                pe.wait_ge(x2_ready, t + 1)
                if t:
                    pe.wait_ge(x2T_by_act, t)
                    pe.wait_ge(x2T_by_dve, t)
                for k in range(M1):
                    last = pe.transpose(bank[x2_bank[k // HALF]][:, (k % HALF) * P:(k % HALF + 1) * P],
                                        x2[:, t % 2, k * P:(k + 1) * P], ident[:])
                    if k == HALF - 1:
                        last.then_inc(x2_turned_low, 1)
                last.then_inc(x2_turned, 1)

            def layer2(t):
                pe.wait_ge(x2T_by_act, t + 1)
                pe.wait_ge(x2T_by_dve, t + 1)
                if t >= 2:
                    pe.wait_ge(y2_copied, t - 1)
                for m in range(M2):
                    for k in range(M1):
                        last = pe.matmul(y2_bank[t % 2][:, m * P:(m + 1) * P], w2[:, k, m * P:(m + 1) * P],
                                         x2T[:, t, k, :], start=(k == 0), stop=(k == M1 - 1),
                                         skip_group_check=True)
                last.then_inc(y2_summed, 1)

            turn_z1(0)
            turn_z1(1)
            pe.wait_ge(w2_loaded, 16)
            for t in range(T):
                turn_x2(t)
                if t + 2 < T:
                    turn_z1(t + 2)
                layer2(t)
            for t in range(T):
                for m in range(M2):
                    if t == 0:
                        pe.wait_ge(z2_ready, m + 1)
                    last = pe.transpose(z2_bank[t][:, m * P:(m + 1) * P], y2[:, m, t * P:(t + 1) * P], ident[:])
                last.then_inc(z2_turned, 1)


_INS = ['r_items', 'r_users', 'r_history_users', 'L0_rec_item_table', 'L0_rec_user_table', 'L0_rec_W1',
        'L0_rec_b1', 'L0_rec_g1', 'L0_rec_be1', 'L0_rec_a1', 'L0_rec_W2', 'L0_rec_b2', 'L0_rec_g2',
        'L0_rec_be2', 'L0_rec_a2', 'L0_rec_W3', 'L0_rec_b3']


def kernel(**inputs):
    import numpy as np
    import concourse.bacc as bacc
    from concourse.bass_utils import run_bass_kernel_spmd

    nc = bacc.Bacc("TRN2", target_bir_lowering=False, num_devices=1)
    arrays, args = {}, []
    for name in _INS:
        a = np.ascontiguousarray(inputs[name])
        arrays[f"in_{name}"] = a
        args.append(nc.dram_tensor(f"in_{name}", a.shape, mybir.dt.from_np(a.dtype), kind="ExternalInput").ap())
    batch = inputs['r_items'].shape[0]
    args.append(nc.dram_tensor("out", (batch, 1), F32, kind="ExternalOutput").ap())
    recommender_kernel(nc, *args)
    r = run_bass_kernel_spmd(nc, [arrays], core_ids=[0])
    return r.results[0]["out"]
```

```python
from contextlib import ExitStack

import concourse.bass as bass
from concourse import mybir

F32 = mybir.dt.float32
I32 = mybir.dt.int32
F32R = mybir.dt.float32r
ALU = mybir.AluOpType
ACT = mybir.ActivationFunctionType
AX = mybir.AxisListType

P = 128
BANK = 512
RING = 16
GROUP = 8
USUAL = 3
WARM_SLOT = 1
WARM_GATES = 6
DICE_EPS = 1e-3
BN_EPS = 1e-5


def recommender_kernel(nc, items, users, history, item_table, user_table, W1, b1, g1, be1, a1,
                       W2, b2, g2, be2, a2, W3, b3, out):
    B, H = history.shape
    n_item, D = item_table.shape
    n_user = user_table.shape[0]
    d_in, F1 = W1.shape
    F2 = W2.shape[1]
    T = B // P
    M1, M2 = F1 // P, F2 // P
    KIN = d_in // P
    ITEMS, HIS, USER = range(KIN)
    HALF = M1 // 2
    PAD = -(-H // GROUP) * GROUP
    LOOPS = -(-H // RING)
    VEC = 3 * M1 + 4 * M2
    assert D == P and KIN == 3 and HALF * P == BANK and F2 == BANK and T == 4

    with ExitStack() as ctx:
        def sb(name, shape, dt=F32):
            return ctx.enter_context(nc.sbuf_tensor(name, shape, dt))

        def sem(name):
            return ctx.enter_context(nc.semaphore(name))

        bank = [ctx.enter_context(nc.psum_tensor(f"bank{i}", [P, BANK], F32)) for i in range(8)]

        raw_users, raw_items = sb("raw_users", [P, T], I32), sb("raw_items", [P, T], I32)
        raw_history = sb("raw_history", [P, T, H], I32)
        from_last_u, from_last_i = sb("from_last_u", [P, T]), sb("from_last_i", [P, T])
        from_last_h = sb("from_last_h", [P, T, H])
        user_rows, item_rows = sb("user_rows", [P, T], I32), sb("item_rows", [P, T], I32)
        wrap_u, wrap_i = sb("wrap_u", [P, T]), sb("wrap_i", [P, T])
        used = sb("used", [P, T, H])
        need_tag = sb("need_tag", [P, T])
        need_code, need_order = sb("need_code", [P, GROUP]), sb("need_order", [P, GROUP])
        ranked = sb("ranked", [P, T, T])
        products = sb("products", [P, 3, T, T])
        ranked_i = sb("ranked_i", [P, T])
        keys = sb("keys", [P, T, PAD])
        n_used, n_last = sb("n_used", [P, T]), sb("n_last", [P, T])
        needed = sb("needed", [T, 1], I32)
        top = sb("top", [P, T, 2, GROUP])
        slot_mask = sb("slot_mask", [P, T, 2, GROUP])
        slot_row = sb("slot_row", [P, T, 2, GROUP], I32)
        user_drawn = sb("user_drawn", [P, T, D])
        user_emb, item_emb = sb("user_emb", [P, T, D]), sb("item_emb", [P, T, D])
        ring = sb("ring", [P, 2, RING, D])
        copied_zw = ring[:, 0, :, :].rearrange("p s d -> p (s d)").rearrange("p (t f) -> p t f", t=T)
        last_row = sb("last_row", [P, D])
        score = sb("score", [P, T, RING])
        last_score = sb("last_score", [P, T])
        diag = sb("diag", [P, 2, RING, P])
        last_diag = sb("last_diag", [P, 2, P])
        ident, zeros = sb("ident", [P, P]), sb("zeros", [P, P])
        minus_half = sb("minus_half", [P, M1])
        w1, w2 = sb("w1", [P, KIN, F1]), sb("w2", [P, M1, F2])
        w2_hi, w2_lo = sb("w2_hi", [P, M1, F2], F32R), sb("w2_lo", [P, M1, F2], F32R)
        w3_diag = sb("w3_diag", [P, M2, P])
        vec_rows, vec = sb("vec_rows", [VEC, P]), sb("vec", [P, VEC])
        scalars, one_minus = sb("scalars", [P, 3]), sb("one_minus", [P, 2])
        xT = sb("xT", [P, KIN, B])
        y1 = sb("y1", [P, M1, B])
        stats1 = sb("stats1", [P, M1, T, 6])
        sig1 = sb("sig1", [P, 2, F1])
        x2 = sb("x2", [P, 2, F1])
        x2T_hi = sb("x2T_hi", [P, T // 2, M1, 2 * P], F32R)
        x2T_lo = sb("x2T_lo", [P, T // 2, M1, 2 * P], F32R)
        y2, z2 = sb("y2", [P, M2, 2 * P]), sb("z2", [P, M2, B])
        stats2 = sb("stats2", [P, M2, T // 2, 6])
        assert RING * P == T * F2
        sig2, gated_z = (diag[:, i, :, :].rearrange("p s b -> p (s b)").rearrange("p (t f) -> p t f", t=T)
                         for i in range(2))
        bn = sb("bn", [P, 12, M1])
        bn1_mv, bn2_mv = sb("bn1_mv", [P, M1, 2]), sb("bn2_mv", [P, M2, 2])
        dice_stats = sb("dice_stats", [P, T, 12])
        dice_mv, dice_var = sb("dice_mv", [P, T, 2]), sb("dice_var", [P, T])
        dice_neg, dice_r, dice_nb = sb("dice_neg", [P, T]), sb("dice_r", [P, T]), sb("dice_nb", [P, T])
        dice2_stats, dice2_mv = sb("dice2_stats", [P, T, 12]), sb("dice2_mv", [P, T, 2])
        dice2_var, dice2_r = sb("dice2_var", [P, T]), sb("dice2_r", [P, T])
        dice2_neg, dice2_nb = sb("dice2_neg", [P, T]), sb("dice2_nb", [P, T])
        plain, shifted, gated = sb("plain", [P, 2]), sb("shifted", [P, T]), sb("gated", [P, T])
        gate2_sum, result = sb("gate2_sum", [P, T]), sb("result", [P, T])
        first_sigmoid = sb("first_sigmoid", [P, 1])

        b1v, g1v, be1v = (vec[:, i * M1:(i + 1) * M1] for i in range(3))
        b2v, g2v, be2v = (vec[:, 3 * M1 + i * M2:3 * M1 + (i + 1) * M2] for i in range(3))
        w3v = vec[:, 3 * M1 + 3 * M2:VEC]
        alpha1, alpha2, bias3 = (scalars[:, i:i + 1] for i in range(3))

        users_loaded, items_loaded = sem("users_loaded"), sem("items_loaded")
        history_loaded, last_row_loaded = sem("history_loaded"), sem("last_row_loaded")
        vectors_loaded, w1_loaded, w2_loaded = sem("vectors_loaded"), sem("w1_loaded"), sem("w2_loaded")
        scalars_loaded = sem("scalars_loaded")
        constants_set, ident_set = sem("constants_set"), sem("ident_set")
        dve_step = sem("dve_step")
        user_rows_ready, item_rows_ready = sem("user_rows_ready"), sem("item_rows_ready")
        ordered, order_and_vectors_turned = sem("ordered"), sem("order_and_vectors_turned")
        keys_ranked, users_ranked = sem("keys_ranked"), sem("users_ranked")
        w3_diag_ready = sem("w3_diag_ready")
        needed_ready = sem("needed_ready")
        users_landed, items_landed = sem("users_landed"), sem("items_landed")
        embs_turned, embs_copied = sem("embs_turned"), sem("embs_copied")
        vec_ready = sem("vec_ready")
        group_sorted = [sem(f"group_sorted{t}") for t in range(T)]
        rows_ready = [sem(f"rows_ready{t}") for t in range(T)]
        landed = [[sem(f"landed{t}_{s}") for s in range(RING)] for t in range(T)]
        scored = [sem(f"scored{t}") for t in range(T)]
        last_scored = sem("last_scored")
        diag_ready = [sem(f"diag_ready{t}") for t in range(T)]
        last_diag_ready = sem("last_diag_ready")
        ring_free = [sem(f"ring_free{t}") for t in range(T)]
        last_row_added, his_copied = sem("last_row_added"), sem("his_copied")
        one_minus_ready = sem("one_minus_ready")
        waits_taken = sem("waits_taken")
        y1_summed, y1_copied = sem("y1_summed"), sem("y1_copied")
        var1_ready, rstd1_ready, affine1_ready = sem("var1_ready"), sem("rstd1_ready"), sem("affine1_ready")
        z1_by_act, z1_by_dve, z1_by_pool = sem("z1_by_act"), sem("z1_by_dve"), sem("z1_by_pool")
        y1_measured, z1_turned = sem("y1_measured"), sem("z1_turned")
        dice_var_ready, dice_r_ready, dice_nb_ready = sem("dice_var_ready"), sem("dice_r_ready"), sem("dice_nb_ready")
        gate1_by_pool = sem("gate1_by_pool")
        sig1_ready, gate1_ready, x2_ready = sem("sig1_ready"), sem("gate1_ready"), sem("x2_ready")
        x2_turned, x2T_hi_ready, x2T_lo_ready = sem("x2_turned"), sem("x2T_hi_ready"), sem("x2T_lo_ready")
        w2_hi_ready, w2_lo_ready = sem("w2_hi_ready"), sem("w2_lo_ready")
        y2_summed, y2_copied = sem("y2_summed"), sem("y2_copied")
        var2_ready, rstd2_ready, affine2_ready = sem("var2_ready"), sem("rstd2_ready"), sem("affine2_ready")
        z2_by_act, z2_by_dve, z2_turned = sem("z2_by_act"), sem("z2_by_dve"), sem("z2_turned")
        dice2_var_ready, dice2_r_ready = sem("dice2_var_ready"), sem("dice2_r_ready")
        dice2_nb_ready, sig2_ready, zw_turned = sem("dice2_nb_ready"), sem("sig2_ready"), sem("zw_turned")
        z2_early_turned, dice2_early = sem("z2_early_turned"), sem("dice2_early")
        dice2_aggregated = sem("dice2_aggregated")
        dice2_measured = sem("dice2_measured")
        plain_by_act, plain_by_pe = sem("plain_by_act"), sem("plain_by_pe")
        result_ready, stored = sem("result_ready"), sem("stored")

        his_bank = [bank[0], bank[1]]
        y1_bank = [(bank[2], bank[3]), (bank[4], bank[5])]
        turn_items, turn_users = bank[6], bank[7]
        z1_bank = [(0, 1), (2, 3), (0, 1), (6, 7)]
        x2_bank = [(4, 5), (6, 7), (4, 5), (4, 5)]
        y2_first = (bank[2], bank[3])
        y2_last = (bank[0], bank[1], bank[6], bank[7])
        z2_bank = (bank[4], bank[5], bank[2], bank[3])
        zw_bank = (bank[0], bank[1], bank[6], bank[4])
        plain_sum = bank[7]
        EARLY = (M2 - 1) * P

        DICE2_GROUPS = [(0, 1), (1, 2), (2, T)]
        W2_CHUNKS = [(), (0, 1, 2), (3, 4, 5), (6, 7)]
        Z1_BY_DVE, Z1_BY_ACT = [(0, 2), (4, 6)], [(1, 3), (5, 7)]
        LO_ORDER = [(0, 0), (1, 0), (0, 1), (1, 1), (2, 0), (2, 1), (3, 0), (3, 1)]
        block = ctx.enter_context(nc.Block())

        @block.sync
        def _(sp):
            sp.dma_start(raw_users[:], users.rearrange("(p t) -> p t", t=T)).then_inc(users_loaded, 16)
            sp.dma_start(raw_history[:], history.rearrange("(p t) h -> p t h", t=T)).then_inc(history_loaded, 16)
            sp.dma_start(raw_items[:], items.rearrange("(p t) -> p t", t=T)).then_inc(items_loaded, 16)
            sp.dma_start(last_row[:], user_table[n_user - 1, :].partition_broadcast(P)).then_inc(last_row_loaded, 16)
            row = 0
            for v in (b1, g1, be1, b2, g2, be2, W3.rearrange("f o -> (f o)")):
                n = v.shape[0] // P
                sp.dma_start(vec_rows[row:row + n, :], v.rearrange("(m p) -> m p", p=P)).then_inc(vectors_loaded, 16)
                row += n
            for i, v in enumerate((a1, a2, b3)):
                sp.dma_start(scalars[:, i:i + 1], v.partition_broadcast(P)).then_inc(scalars_loaded, 16)
            sp.wait_ge(users_landed, 16 * T)
            sp.dma_start(w1[:], W1.rearrange("(k p) f -> p k f", p=P)).then_inc(w1_loaded, 16)
            sp.wait_ge(w1_loaded, 16)
            sp.dma_start(w2[:], W2.rearrange("(k p) f -> p k f", p=P)).then_inc(w2_loaded, 16)
            sp.wait_ge(result_ready, 1)
            sp.dma_start(out.rearrange("(p t) o -> p (t o)", t=T), result[:]).then_inc(stored, 16)
            sp.wait_ge(stored, 16)

        @block.gpsimd
        def _(pool):
            pool.wait_ge(constants_set, 1)
            nc.gpsimd.affine_select(out=ident[:], in_=zeros[:], compare_op=ALU.not_equal, fill=1.0, base=0,
                                    pattern=[[-1, P]], channel_multiplier=1).then_inc(ident_set, 1)

            def gather(dst, table, rows):
                return nc.gpsimd.indirect_dma_start(dst, None, table[:, :],
                                                    bass.IndirectOffsetOnAxis(ap=rows, axis=0))

            pool.wait_ge(user_rows_ready, 1)
            for t in range(T):
                gather(user_drawn[:, t, :], user_table, user_rows[:, t:t + 1]).then_inc(users_landed, 16)
            pool.wait_ge(item_rows_ready, 1)
            for t in range(T):
                gather(item_emb[:, t, :], item_table, item_rows[:, t:t + 1]).then_inc(items_landed, 16)

            pool.wait_ge(needed_ready, 1)
            needs = [pool.value_load(needed[t:t + 1, 0:1], min_val=0, max_val=H) for t in range(T)]
            for t in range(T):
                par, need = t % 2, needs[t]

                def slot(i, s):
                    group = s // GROUP
                    pool.wait_ge(rows_ready[t], 2 * i + group + 1)
                    pool.wait_ge(ring_free[t], RING * i + s + 1)
                    pool.sem_inc(waits_taken, 1)
                    gather(ring[:, par, s, :], user_table,
                           slot_row[:, t, group, s % GROUP:s % GROUP + 1]).then_inc(landed[t][s], 16)

                def iteration(i, s=0):
                    with pool.If(need > RING * i + s):
                        slot(i, s)
                        if s + 1 < RING:
                            iteration(i, s + 1)

                with pool.Fori(0, USUAL) as i:
                    iteration(i)
                with pool.If(need > RING * USUAL):
                    with pool.Fori(USUAL, LOOPS) as i:
                        iteration(i)

            def rsqrt(dst, src, n):
                return nc.gpsimd.tensor_tensor(dst, src, minus_half[:, 0:n], ALU.pow)

            def normalize1(m):
                nc.gpsimd.tensor_scalar(y1[:, m, 2 * P:B], y1[:, m, 2 * P:B], bn[:, 4, m:m + 1],
                                        bn[:, 5, m:m + 1], ALU.mult, ALU.add).then_inc(z1_by_pool, 1)

            def sigmoid_operands(lo, hi, n, var_ready, var, r, r_ready, neg, nb, nb_ready):
                pool.wait_ge(var_ready, n)
                rsqrt(r[:, lo:hi], var[:, lo:hi], hi - lo).then_inc(r_ready, 1)
                pool.wait_ge(r_ready, n)
                nc.gpsimd.tensor_tensor(nb[:, lo:hi], neg[:, lo:hi], r[:, lo:hi], ALU.mult).then_inc(nb_ready, 1)

            dice1 = (dice_var_ready, dice_var, dice_r, dice_r_ready, dice_neg, dice_nb, dice_nb_ready)
            dice2 = (dice2_var_ready, dice2_var, dice2_r, dice2_r_ready, dice2_neg, dice2_nb, dice2_nb_ready)

            pool.wait_ge(constants_set, 2)
            for h in range(2):
                pool.wait_ge(var1_ready, h + 1)
                rsqrt(bn[:, 3, h * HALF:(h + 1) * HALF], bn[:, 2, h * HALF:(h + 1) * HALF],
                      HALF).then_inc(rstd1_ready, 1)
            pool.wait_ge(y1_copied, T)
            pool.wait_ge(affine1_ready, 2)
            for m in range(0, 3):
                normalize1(m)
            sigmoid_operands(0, 1, 1, *dice1)
            for m in range(3, 5):
                normalize1(m)
            sigmoid_operands(1, 2, 2, *dice1)
            pool.wait_ge(sig1_ready, 3)
            nc.gpsimd.tensor_scalar(sig1[:, 1, 0:BANK], sig1[:, 1, 0:BANK], one_minus[:, 0:1], alpha1,
                                    ALU.mult, ALU.add).then_inc(gate1_by_pool, 1)
            for m in range(5, M1):
                normalize1(m)
            for t in range(2, T):
                sigmoid_operands(t, t + 1, t + 1, *dice1)
            for m in range(M2):
                pool.wait_ge(var2_ready, m + 1)
                rsqrt(bn[:, 9, m:m + 1], bn[:, 8, m:m + 1], 1).then_inc(rstd2_ready, 1)
            for n, (lo, hi) in enumerate(DICE2_GROUPS):
                sigmoid_operands(lo, hi, n + 1, *dice2)

        @block.vector
        def _(dve):
            steps = [0]

            def step(ins):
                steps[0] += 1
                ins.then_inc(dve_step, 1)
                dve.wait_ge(dve_step, steps[0])

            nc.vector.memset(zeros[:], 0.0).then_inc(constants_set, 1)
            nc.vector.memset(minus_half[:], -0.5).then_inc(constants_set, 1)
            nc.vector.memset(keys[:], 0.0)
            for t in range(T):
                nc.vector.memset(need_tag[:, t:t + 1], t / GROUP)
            step(nc.vector.memset(need_code[:], -1.0))

            def distance(dst, wrap, raw, n):
                nc.vector.tensor_scalar(wrap, raw, 0.0, -float(n), ALU.is_lt, ALU.mult)
                return nc.vector.tensor_scalar(dst, raw, -1.0, float(n - 1), ALU.mult, ALU.add)

            def wrapped(dst, wrap):
                return nc.vector.tensor_tensor(dst, dst, wrap, ALU.add)

            def clamped(dst, n):
                return nc.vector.tensor_scalar(dst, dst, 0.0, float(n - 1), ALU.max, ALU.min)

            dve.wait_ge(users_loaded, 16)
            step(distance(from_last_u[:], wrap_u[:], raw_users[:], n_user))
            step(wrapped(from_last_u[:], wrap_u[:]))
            step(clamped(from_last_u[:], n_user))
            nc.vector.tensor_scalar(user_rows[:], from_last_u[:], -1.0, float(n_user - 1),
                                    ALU.mult, ALU.add).then_inc(user_rows_ready, 1)
            dve.wait_ge(history_loaded, 16)
            distance(from_last_h[:], used[:], raw_history[:], n_user)
            dve.wait_ge(items_loaded, 16)
            step(distance(from_last_i[:], wrap_i[:], raw_items[:], n_item))
            wrapped(from_last_i[:], wrap_i[:])
            step(wrapped(from_last_h[:], used[:]))
            clamped(from_last_i[:], n_item)
            step(clamped(from_last_h[:], n_user))
            step(nc.vector.tensor_scalar(used[:], from_last_h[:], 1.0, None, ALU.min))
            step(nc.vector.tensor_reduce(n_used[:], used[:], AX.X, ALU.add))
            step(nc.vector.tensor_tensor(need_code[:, 0:T], n_used[:], need_tag[:], ALU.add))
            nc.vector.max(need_order[:], need_code[:]).then_inc(ordered, 1)
            dve.wait_ge(ordered, 1)
            over_ranks = lambda x: x.unsqueeze(1).to_broadcast([P, T, T])
            step(nc.vector.tensor_tensor(ranked[:], need_order[:, 0:T].unsqueeze(2).to_broadcast([P, T, T]),
                                         over_ranks(need_code[:, 0:T]), ALU.is_equal))
            step(nc.vector.tensor_tensor(products[:, 0, :, :], ranked[:], over_ranks(from_last_i[:]), ALU.mult))
            step(nc.vector.tensor_reduce(ranked_i[:], products[:, 0, :, :], AX.X, ALU.add))
            nc.vector.tensor_scalar(item_rows[:], ranked_i[:], -1.0, float(n_item - 1),
                                    ALU.mult, ALU.add).then_inc(item_rows_ready, 1)

            def rank(dst, src, tiles, done):
                for j in range(T):
                    for n, t in enumerate(tiles):
                        if j == 0:
                            ins = nc.vector.tensor_scalar(dst(t), src(j), ranked[:, t, j:j + 1], None, ALU.mult)
                        else:
                            dve.wait_ge(done, ranks[done.name] + (j - 1) * len(tiles) + n + 1)
                            ins = nc.vector.scalar_tensor_tensor(out=dst(t), in0=src(j), scalar=ranked[:, t, j:j + 1],
                                                                 in1=dst(t), op0=ALU.mult, op1=ALU.add)
                        ins.then_inc(done, 1)
                ranks[done.name] += T * len(tiles)
                dve.wait_ge(done, ranks[done.name])

            ranks = {keys_ranked.name: 0, users_ranked.name: 0}

            def rank_keys(tiles):
                rank(lambda t: keys[:, t, 0:H], lambda j: from_last_h[:, j, :], tiles, keys_ranked)

            def rank_users(tiles):
                rank(lambda t: user_emb[:, t, :], lambda j: user_drawn[:, j, :], tiles, users_ranked)

            def sort(t, group, n):
                dve.wait_ge(group_sorted[t], 2 * n)
                dve.sem_inc(waits_taken, 1)
                sort_pass(t, group, n)

            def sort_pass(t, group, n):
                nc.vector.max(top[:, t, group, :], keys[:, t, :]).then_inc(group_sorted[t], 1)
                dve.wait_ge(group_sorted[t], 2 * n + 1)
                nc.vector.tensor_scalar(slot_row[:, t, group, :], top[:, t, group, :], -1.0,
                                        float(n_user - 1), ALU.mult, ALU.add).then_inc(rows_ready[t], 1)
                nc.vector.tensor_scalar(slot_mask[:, t, group, :], top[:, t, group, :], 1.0, None, ALU.min)
                nc.vector.match_replace(keys[:, t, :], top[:, t, group, :], keys[:, t, :],
                                        0.0).then_inc(group_sorted[t], 1)

            def first_sorts(t):
                sort_pass(t, 0, 0)
                sort(t, 1, 1)

            rank_keys([0])
            dve.wait_ge(order_and_vectors_turned, 1)
            nc.vector.tensor_reduce(needed[:], bank[2][0:T, 0:P], AX.X, ALU.max).then_inc(needed_ready, 1)
            first_sorts(0)
            step(nc.vector.tensor_tensor(products[:, 1, :, :], ranked[:], over_ranks(n_used[:]), ALU.mult))
            step(nc.vector.tensor_reduce(n_last[:], products[:, 1, :, :], AX.X, ALU.add))
            step(nc.vector.tensor_scalar(n_last[:], n_last[:], -1.0, float(H), ALU.mult, ALU.add))
            dve.wait_ge(users_landed, 16 * T)
            rank_users([0])
            rank_keys([1, 2, 3])
            rank_users([1, 2, 3])
            dve.wait_ge(scalars_loaded, 48)
            nc.vector.tensor_scalar(one_minus[:], scalars[:, 0:2], -1.0, 1.0, ALU.mult,
                                    ALU.add).then_inc(one_minus_ready, 1)
            dve.wait_ge(order_and_vectors_turned, 2)
            nc.vector.tensor_copy(vec[:], bank[3][:, 0:VEC]).then_inc(vec_ready, 1)
            dve.wait_ge(last_row_loaded, 16)
            dve.wait_ge(needed_ready, 1)

            def measure1(t):
                dve.wait_ge(y1_copied, t + 1)
                for m in range(M1):
                    nc.vector.bn_stats(stats1[:, m, t, :], y1[:, m, t * P:(t + 1) * P])

            needs = [dve.value_load(needed[t:t + 1, 0:1], min_val=0, max_val=H) for t in range(T)]
            for t in range(T):
                par, need = t % 2, needs[t]
                nc.vector.tensor_tensor_reduce(last_diag[:, par, :], last_row[:], user_emb[:, t, :],
                                               n_last[:, t:t + 1], 0.0, ALU.mult, ALU.add,
                                               last_score[:, t:t + 1]).then_inc(last_scored, 1)
                if t + 1 < T:
                    first_sorts(t + 1)
                if t:
                    measure1(t - 1)
                for k in W2_CHUNKS[t]:
                    dve.wait_ge(w2_hi_ready, k + 1)
                    nc.vector.tensor_tensor(w2_lo[:, k, :], w2[:, k, :], w2_hi[:, k, :].bitcast(F32),
                                            ALU.subtract).then_inc(w2_lo_ready, 1)

                def slot(i, s):
                    group = s // GROUP
                    dve.wait_ge(group_sorted[t], 2 * (2 * i + group) + 2)
                    dve.wait_ge(landed[t][s], 16 * (i + 1))
                    nc.vector.tensor_tensor_reduce(
                        diag[:, par, s, :], ring[:, par, s, :], user_emb[:, t, :],
                        slot_mask[:, t, group, s % GROUP:s % GROUP + 1], 0.0, ALU.mult, ALU.add,
                        score[:, t, s:s + 1]).then_inc(scored[t], 1)

                def iteration(i, s=0):
                    with dve.If(need > RING * i + s):
                        slot(i, s)
                        if (s + 1) % GROUP == 0:
                            group = s // GROUP
                            with dve.If(need > RING * (i + 1) + GROUP * group):
                                sort(t, group, 2 * i + 2 + group)
                        if s + 1 < RING:
                            iteration(i, s + 1)

                with dve.Fori(0, USUAL) as i:
                    iteration(i)
                with dve.If(need > RING * USUAL):
                    with dve.Fori(USUAL, LOOPS) as i:
                        iteration(i)

            def norm_variance(mv, lo, hi, base, var_ready):
                nc.vector.tensor_scalar(bn[:, base + 2, lo:hi], mv[:, lo:hi, 1], BN_EPS, None,
                                        ALU.add).then_inc(var_ready, 1)

            def norm_mean(mv, lo, hi, base, bias):
                row = lambda n: bn[:, base + n, lo:hi]
                step(nc.vector.tensor_tensor(row(0), mv[:, lo:hi, 0], bias[:, lo:hi], ALU.add))
                return nc.vector.tensor_tensor(row(1), bias[:, lo:hi], row(0), ALU.subtract)

            for h in range(2):
                lo, hi = h * HALF, (h + 1) * HALF
                dve.wait_ge(y1_summed, T + h)
                for m in range(lo, hi):
                    last = nc.vector.bn_stats(stats1[:, m, T - 1, :],
                                              y1_bank[(T - 1) % 2][h][:, (m - lo) * P:(m - lo + 1) * P])
                last.then_inc(y1_measured, 1)
                dve.wait_ge(y1_measured, h + 1)
                for m in range(lo, hi):
                    last = nc.vector.bn_aggr(bn1_mv[:, m, :], stats1[:, m, :, :].rearrange("p t c -> p (t c)"))
                step(last)
                norm_variance(bn1_mv, lo, hi, 0, var1_ready)
                if h == 0:
                    step(norm_mean(bn1_mv, lo, hi, 0, b1v))
            for h in range(2):
                lo, hi = h * HALF, (h + 1) * HALF
                dve.wait_ge(rstd1_ready, h + 1)
                step(nc.vector.tensor_tensor(bn[:, 4, lo:hi], bn[:, 3, lo:hi], g1v[:, lo:hi], ALU.mult))
                step(nc.vector.tensor_tensor(bn[:, 0, lo:hi], bn[:, 1, lo:hi], bn[:, 4, lo:hi], ALU.mult))
                nc.vector.tensor_tensor(bn[:, 5, lo:hi], bn[:, 0, lo:hi], be1v[:, lo:hi],
                                        ALU.add).then_inc(affine1_ready, 1)
                if h == 0:
                    step(norm_mean(bn1_mv, HALF, M1, 0, b1v))
                dve.wait_ge(affine1_ready, h + 1)
                for m in Z1_BY_DVE[h]:
                    nc.vector.tensor_scalar(y1[:, m, 0:2 * P], y1[:, m, 0:2 * P], bn[:, 4, m:m + 1],
                                            bn[:, 5, m:m + 1], ALU.mult, ALU.add).then_inc(z1_by_dve, 1)

            def dice_operands(mv, t, n, neg, var, var_ready):
                nc.vector.tensor_scalar(neg[:, t:t + 1], mv[:, t, 0:1], -1.0, None, ALU.mult)
                nc.vector.tensor_scalar(var[:, t:t + 1], mv[:, t, 1:2], float(n), n * DICE_EPS,
                                        ALU.mult, ALU.add).then_inc(var_ready, 1)

            def dice1_measure(t):
                for h in range(2):
                    dve.wait_ge(z1_turned, 2 * t + h + 1)
                    last = nc.vector.bn_stats(dice_stats[:, t, 6 * h:6 * h + 6], bank[z1_bank[t][h]][:])
                step(last)
                step(nc.vector.bn_aggr(dice_mv[:, t, :], dice_stats[:, t, :]))
                dice_operands(dice_mv, t, F1, dice_neg, dice_var, dice_var_ready)

            def dice1_apply(t):
                for h in range(2):
                    half = slice(h * BANK, (h + 1) * BANK)
                    if t == 0:
                        dve.wait_ge(sig1_ready, h + 1)
                        step(nc.vector.tensor_scalar(sig1[:, 0, half], sig1[:, 0, half], one_minus[:, 0:1], alpha1,
                                                     ALU.mult, ALU.add))
                    elif (t, h) == (1, 0):
                        dve.wait_ge(gate1_by_pool, 1)
                    else:
                        dve.wait_ge(gate1_ready, 2 * (t - 1) + h)
                    if t >= 2:
                        dve.wait_ge(x2_turned, 2 * (t - 2) + h + 1)
                    nc.vector.tensor_tensor(x2[:, t % 2, half], sig1[:, t % 2, half], bank[z1_bank[t][h]][:],
                                            ALU.mult).then_inc(x2_ready, 1)

            def x2T_low(t, h):
                part = (slice(None), t // 2, slice(h * HALF, (h + 1) * HALF), slice(t % 2 * P, (t % 2 + 1) * P))
                dve.wait_ge(x2T_hi_ready, LO_ORDER.index((t, h)) + 1)
                nc.vector.tensor_tensor(x2T_lo[part], bank[x2_bank[t][h]][:].rearrange("p (k b) -> p k b", b=P),
                                        x2T_hi[part].bitcast(F32), ALU.subtract).then_inc(x2T_lo_ready, 1)

            for pair in range(2):
                for t in 2 * pair, 2 * pair + 1:
                    dice1_measure(t)
                for t in 2 * pair, 2 * pair + 1:
                    dice1_apply(t)
                for t, h in LO_ORDER[4 * pair:4 * pair + 4]:
                    x2T_low(t, h)

            def dice2_measure_early(t):
                dve.wait_ge(z2_early_turned, t + 1)
                nc.vector.bn_stats(dice2_stats[:, t, 0:6], z2_bank[t][:, 0:EARLY]).then_inc(dice2_early, 1)

            dve.wait_ge(y2_copied, 1)
            for m in range(M2):
                nc.vector.bn_stats(stats2[:, m, 0, :], y2[:, m, :])
            scale2 = lambda m: bn[:, 10, m:m + 1]
            shift2 = lambda m: bn[:, 11, m:m + 1]
            for m in range(M2):
                dve.wait_ge(y2_summed, m + 2)
                step(nc.vector.bn_stats(stats2[:, m, 1, :], y2_last[m][:, 0:2 * P]))
                step(nc.vector.bn_aggr(bn2_mv[:, m, :], stats2[:, m, :, :].rearrange("p t c -> p (t c)")))
                norm_variance(bn2_mv, m, m + 1, 6, var2_ready)
                step(norm_mean(bn2_mv, m, m + 1, 6, b2v))
                if m == M2 - 1:
                    dice2_measure_early(0)
                dve.wait_ge(rstd2_ready, m + 1)
                step(nc.vector.tensor_tensor(scale2(m), bn[:, 9, m:m + 1], g2v[:, m:m + 1], ALU.mult))
                nc.vector.scalar_tensor_tensor(out=shift2(m), in0=bn[:, 7, m:m + 1], scalar=scale2(m),
                                               in1=be2v[:, m:m + 1], op0=ALU.mult,
                                               op1=ALU.add).then_inc(affine2_ready, 1)
                dve.wait_ge(affine2_ready, m + 1)
                nc.vector.tensor_scalar(z2[:, m, 0:2 * P], y2[:, m, :], scale2(m), shift2(m), ALU.mult,
                                        ALU.add).then_inc(z2_by_dve, 1)

            def dice2_measure(t):
                dve.wait_ge(z2_turned, t + 1)
                nc.vector.bn_stats(dice2_stats[:, t, 6:12], z2_bank[t][:, EARLY:F2]).then_inc(dice2_measured, 1)

            def dice2_aggregate(t):
                dve.wait_ge(dice2_measured, t + 1)
                nc.vector.bn_aggr(dice2_mv[:, t, :], dice2_stats[:, t, :]).then_inc(dice2_aggregated, 1)

            def dice2_operands(lo, hi):
                dve.wait_ge(dice2_aggregated, hi)
                nc.vector.tensor_scalar(dice2_neg[:, lo:hi], dice2_mv[:, lo:hi, 0], -1.0, None, ALU.mult)
                nc.vector.tensor_scalar(dice2_var[:, lo:hi], dice2_mv[:, lo:hi, 1], float(F2), F2 * DICE_EPS,
                                        ALU.mult, ALU.add).then_inc(dice2_var_ready, 1)

            dice2_measure_early(1)
            dice2_measure(0)
            dice2_measure_early(2)
            dice2_aggregate(0)
            dice2_measure(1)
            dice2_operands(*DICE2_GROUPS[0])
            dice2_aggregate(1)
            dice2_measure_early(3)
            dice2_operands(*DICE2_GROUPS[1])
            for t in 2, 3:
                dice2_measure(t)
            for t in 2, 3:
                dice2_aggregate(t)
            dice2_operands(*DICE2_GROUPS[2])

            def dice2_gate(t):
                dve.wait_ge(sig2_ready, t + 1)
                dve.wait_ge(zw_turned, t + 1)
                nc.vector.tensor_tensor_reduce(gated_z[:, t, :], sig2[:, t, :], zw_bank[t][:], 1.0, 0.0,
                                               ALU.mult, ALU.add, gated[:, t:t + 1])

            dve.wait_ge(plain_by_act, 2)
            nc.vector.tensor_scalar(shifted[:, 0:2], plain[:], alpha2, bias3, ALU.mult, ALU.add)
            for t in range(T):
                dice2_gate(t)
            dve.wait_ge(plain_by_pe, 2)
            step(nc.vector.tensor_scalar(shifted[:, 2:T], plain_sum[:, 2:T], alpha2, bias3, ALU.mult, ALU.add))
            step(nc.vector.scalar_tensor_tensor(out=gate2_sum[:], in0=gated[:], scalar=one_minus[:, 1:2],
                                                in1=shifted[:], op0=ALU.mult, op1=ALU.add))
            step(nc.vector.tensor_tensor(products[:, 2, :, :], ranked[:].rearrange("p t j -> p j t"),
                                         over_ranks(gate2_sum[:]), ALU.mult))
            nc.vector.tensor_reduce(result[:], products[:, 2, :, :], AX.X, ALU.add).then_inc(result_ready, 1)

        @block.scalar
        def _(act):
            act.wait_ge(constants_set, 1)
            nc.scalar.activation(first_sigmoid[:], zeros[:, 0:1], ACT.Sigmoid)
            act.wait_ge(embs_turned, 1)
            nc.scalar.copy(xT[:, USER, :], turn_users[:]).then_inc(embs_copied, 1)
            act.wait_ge(embs_turned, 2)
            nc.scalar.copy(xT[:, ITEMS, :], turn_items[:]).then_inc(embs_copied, 1)
            act.wait_ge(vec_ready, 1)
            for m in range(M2):
                last = nc.scalar.mul(w3_diag[:, m, :], ident[:], w3v[:, m:m + 1])
            last.then_inc(w3_diag_ready, 1)
            act.wait_ge(needed_ready, 1)

            def y1_copy(t):
                act.wait_ge(y1_summed, t + 1)
                for h in range(2):
                    if t == T - 1:
                        act.wait_ge(y1_measured, h + 1)
                    last = nc.scalar.copy(y1[:, h * HALF:(h + 1) * HALF, t * P:(t + 1) * P],
                                          y1_bank[t % 2][h][:].rearrange("p (m b) -> p m b", b=P))
                last.then_inc(y1_copied, 1)

            needs = [act.value_load(needed[t:t + 1, 0:1], min_val=0, max_val=H) for t in range(T)]
            for t in range(T):
                par, need = t % 2, needs[t]
                act.wait_ge(last_scored, t + 1)
                nc.scalar.mul(last_diag[:, par, :], ident[:], last_score[:, t:t + 1]).then_inc(last_diag_ready, 1)
                if t:
                    y1_copy(t - 1)
                if W2_CHUNKS[t]:
                    act.wait_ge(w2_loaded, 16)
                for k in W2_CHUNKS[t]:
                    nc.scalar.copy(w2_hi[:, k, :], w2[:, k, :]).then_inc(w2_hi_ready, 1)

                def slot(i, s):
                    act.wait_ge(scored[t], RING * i + s + 1)
                    nc.scalar.mul(diag[:, par, s, :], ident[:], score[:, t, s:s + 1]).then_inc(diag_ready[t], 1)

                def iteration(i, s=0):
                    with act.If(need > RING * i + s):
                        slot(i, s)
                        if s + 1 < RING:
                            iteration(i, s + 1)

                with act.Fori(0, USUAL) as i:
                    iteration(i)
                with act.If(need > RING * USUAL):
                    with act.Fori(USUAL, LOOPS) as i:
                        iteration(i)
                act.wait_ge(last_row_added, t + 1)
                act.wait_ge(ring_free[t], need + RING)
                nc.scalar.copy(xT[:, HIS, t * P:(t + 1) * P], his_bank[par][:, 0:P]).then_inc(his_copied, 1)

            y1_copy(T - 1)
            for h in range(2):
                act.wait_ge(affine1_ready, h + 1)
                for m in Z1_BY_ACT[h]:
                    nc.scalar.activation(y1[:, m, 0:2 * P], y1[:, m, 0:2 * P], ACT.Identity,
                                         bias=bn[:, 5, m:m + 1], scale=bn[:, 4, m:m + 1]).then_inc(z1_by_act, 1)

            def dice1_sigmoid(t):
                act.wait_ge(dice_nb_ready, t + 1)
                for h in range(2):
                    half = slice(h * BANK, (h + 1) * BANK)
                    if t >= 2:
                        act.wait_ge(x2_ready, 2 * (t - 2) + h + 1)
                    nc.scalar.activation(sig1[:, t % 2, half], bank[z1_bank[t][h]][:], ACT.Sigmoid,
                                         bias=dice_nb[:, t:t + 1], scale=dice_r[:, t:t + 1]).then_inc(sig1_ready, 1)
                    if t and (t, h) != (1, 0):
                        act.wait_ge(sig1_ready, 2 * t + h + 1)
                        nc.scalar.activation(sig1[:, t % 2, half], sig1[:, t % 2, half], ACT.Identity,
                                             bias=alpha1, scale=one_minus[:, 0:1]).then_inc(gate1_ready, 1)

            def x2T_high(t, h):
                act.wait_ge(x2_turned, 2 * t + h + 1)
                nc.scalar.copy(x2T_hi[:, t // 2, h * HALF:(h + 1) * HALF, t % 2 * P:(t % 2 + 1) * P],
                               bank[x2_bank[t][h]][:].rearrange("p (k b) -> p k b", b=P)).then_inc(x2T_hi_ready, 1)

            act.wait_ge(one_minus_ready, 1)
            for pair in range(2):
                for t in 2 * pair, 2 * pair + 1:
                    dice1_sigmoid(t)
                for t, h in LO_ORDER[4 * pair:4 * pair + 4]:
                    x2T_high(t, h)
            act.wait_ge(y2_summed, 1)
            for i in range(2):
                last = nc.scalar.copy(y2[:, 2 * i:2 * i + 2, :],
                                      y2_first[i][:].rearrange("p (m b) -> p m b", b=2 * P))
            last.then_inc(y2_copied, 1)
            for m in range(M2):
                act.wait_ge(affine2_ready, m + 1)
                nc.scalar.activation(z2[:, m, 2 * P:B], y2_last[m][:, 0:2 * P], ACT.Identity,
                                     bias=bn[:, 11, m:m + 1], scale=bn[:, 10, m:m + 1]).then_inc(z2_by_act, 1)
            for t in 0, 1:
                act.wait_ge(zw_turned, t + 1)
                nc.scalar.activation(copied_zw[:, t, :], zw_bank[t][:], ACT.Copy,
                                     accum_out=plain[:, t:t + 1]).then_inc(plain_by_act, 1)
            for t in range(T):
                act.wait_ge(dice2_nb_ready, 1 + [t < hi for _, hi in DICE2_GROUPS].index(True))
                nc.scalar.activation(sig2[:, t, :], z2_bank[t][:], ACT.Sigmoid, bias=dice2_nb[:, t:t + 1],
                                     scale=dice2_r[:, t:t + 1]).then_inc(sig2_ready, 1)

        @block.tensor
        def _(pe):
            pe.wait_ge(ident_set, 1)

            def warm_up(where, n):
                for _ in range(n):
                    pe.matmul(where[:, 0:P], ident[:], zeros[:], start=True, stop=True)

            def open_ring(t):
                pe.matmul(his_bank[t % 2][:, 0:P], ident[:], zeros[:], start=True, stop=False,
                          skip_group_check=True).then_inc(ring_free[t], RING)

            open_ring(0)
            open_ring(1)
            pe.wait_ge(ordered, 1)
            pe.transpose(bank[2][0:T, 0:P], need_order[:, 0:T], ident[:]).then_inc(order_and_vectors_turned, 1)
            pe.wait_ge(vectors_loaded, 16 * 7)
            pe.transpose(bank[3][:, 0:VEC], vec_rows[:], ident[0:VEC, 0:VEC]).then_inc(order_and_vectors_turned, 1)
            pe.wait_ge(users_ranked, T * T)
            for t in range(T):
                last = pe.transpose(turn_users[:, t * P:(t + 1) * P], user_emb[:, t, :], ident[:])
            last.then_inc(embs_turned, 1)
            pe.wait_ge(needed_ready, 1)
            pe.wait_ge(items_landed, 16 * T)
            for t in range(T):
                last = pe.transpose(turn_items[:, t * P:(t + 1) * P], item_emb[:, t, :], ident[:])
            last.then_inc(embs_turned, 1)
            needs = [pe.value_load(needed[t:t + 1, 0:1], min_val=0, max_val=H) for t in range(T)]
            pe.wait_ge(vec_ready, 1)
            pe.wait_ge(embs_copied, 2)
            pe.wait_ge(w1_loaded, 16)

            def layer1(t, ks, halves=(0, 1)):
                for h in halves:
                    for k in ks:
                        for j in range(HALF):
                            m = h * HALF + j
                            last = pe.matmul(y1_bank[t % 2][h][:, j * P:(j + 1) * P], w1[:, k, m * P:(m + 1) * P],
                                             xT[:, k, t * P:(t + 1) * P], start=(k == ITEMS and j == 0),
                                             stop=(k == HIS), skip_group_check=True)
                return last

            for t in range(T):
                par, need = t % 2, needs[t]
                if t:
                    pe.wait_ge(his_copied, t)
                    if t + 1 < T:
                        open_ring(t + 1)
                    layer1(t - 1, (HIS,)).then_inc(y1_summed, 1)
                if t >= 2:
                    pe.wait_ge(y1_copied, t - 1)
                layer1(t, (ITEMS, USER))
                pe.wait_ge(last_diag_ready, t + 1)
                pe.matmul(his_bank[par][:, 0:P], last_row[:], last_diag[:, par, :], start=False, stop=False,
                          skip_group_check=True).then_inc(last_row_added, 1)

                def slot(i, s):
                    pe.wait_ge(diag_ready[t], RING * i + s + 1)
                    pe.matmul(his_bank[par][:, 0:P], ring[:, par, s, :], diag[:, par, s, :], start=False,
                              stop=False, skip_group_check=True).then_inc(ring_free[t], 1)
                    if t == T - 1:
                        warm_up(turn_items, WARM_SLOT)

                def iteration(i, s=0):
                    with pe.If(need > RING * i + s):
                        slot(i, s)
                        if s + 1 < RING:
                            iteration(i, s + 1)

                with pe.Fori(0, USUAL) as i:
                    iteration(i)
                with pe.If(need > RING * USUAL):
                    with pe.Fori(USUAL, LOOPS) as i:
                        iteration(i)
            pe.wait_ge(his_copied, T)
            for h in range(2):
                layer1(T - 1, (HIS,), (h,)).then_inc(y1_summed, 1)

            def turn_z1(t):
                for h in range(2):
                    if t == 2:
                        pe.wait_ge(x2_ready, h + 1)
                    elif t == 3:
                        pe.wait_ge(x2T_lo_ready, LO_ORDER.index((1, h)) + 1)
                    for j in range(HALF):
                        m = h * HALF + j
                        if t == 0 and m in Z1_BY_DVE[h]:
                            pe.wait_ge(z1_by_dve, (Z1_BY_DVE[0] + Z1_BY_DVE[1]).index(m) + 1)
                        elif t == 0:
                            pe.wait_ge(z1_by_act, (Z1_BY_ACT[0] + Z1_BY_ACT[1]).index(m) + 1)
                        elif t == 2:
                            pe.wait_ge(z1_by_pool, m + 1)
                        last = pe.transpose(bank[z1_bank[t][h]][:, j * P:(j + 1) * P],
                                            y1[:, m, t * P:(t + 1) * P], ident[:])
                    last.then_inc(z1_turned, 1)

            def turn_x2(t):
                for h in range(2):
                    pe.wait_ge(x2_ready, 2 * t + h + 1)
                    if t >= 2:
                        before = 0 if t == 2 else 2
                        pe.wait_ge(x2T_lo_ready, LO_ORDER.index((before, h)) + 1)
                    for j in range(HALF):
                        k = h * HALF + j
                        last = pe.transpose(bank[x2_bank[t][h]][:, j * P:(j + 1) * P],
                                            x2[:, t % 2, k * P:(k + 1) * P], ident[:])
                    last.then_inc(x2_turned, 1)

            def layer2(pair, m, h, dst, start):
                pe.wait_ge(x2T_lo_ready, LO_ORDER.index((2 * pair + 1, h)) + 1)
                for k in range(h * HALF, (h + 1) * HALF):
                    for w, x in ((w2_hi, x2T_hi), (w2_hi, x2T_lo), (w2_lo, x2T_hi)):
                        last = pe.matmul(dst, w[:, k, m * P:(m + 1) * P], x[:, pair, k, :],
                                         start=(start and k == 0 and w is w2_hi and x is x2T_hi),
                                         stop=(k == M1 - 1 and w is w2_lo), skip_group_check=True)
                return last

            for t in 0, 1:
                turn_z1(t)
            warm_up(bank[4], WARM_GATES)
            for t in 0, 1:
                turn_x2(t)
            turn_z1(2)
            pe.wait_ge(w2_lo_ready, M1)
            for h in range(2):
                for m in range(M2):
                    last = layer2(0, m, h, y2_first[m // 2][:, m % 2 * 2 * P:(m % 2 + 1) * 2 * P], m % 2 == 0)
                    if h == 0 and m == 0:
                        turn_z1(3)
                    if h == 1 and m in (0, 2):
                        turn_x2(2 + m // 2)
            last.then_inc(y2_summed, 1)
            for m in range(M2):
                for h in range(2):
                    last = layer2(1, m, h, y2_last[m][:, 0:2 * P], True)
                last.then_inc(y2_summed, 1)
            pe.wait_ge(x2T_lo_ready, 2 * T)
            pe.wait_ge(y2_copied, 1)

            def turn_z2(t, ms, stage):
                for m in ms:
                    pe.wait_ge(z2_by_dve if t < 2 else z2_by_act, m + 1)
                    z = z2[:, m, t * P:(t + 1) * P]
                    if stage is z2_bank:
                        last = pe.transpose(z2_bank[t][:, m * P:(m + 1) * P], z, ident[:])
                    else:
                        last = pe.matmul(zw_bank[t][:, m * P:(m + 1) * P], z, w3_diag[:, m, :],
                                         start=(m == 0), stop=(m == M2 - 1), skip_group_check=True)
                return last

            early, late = range(M2 - 1), range(M2 - 1, M2)
            for t in range(T):
                turn_z2(t, early, z2_bank).then_inc(z2_early_turned, 1)
            pe.wait_ge(w3_diag_ready, 1)
            for t in 0, 1:
                turn_z2(t, early, zw_bank)
            for t in range(T):
                pe.wait_ge(dice2_early, t + 1)
                turn_z2(t, late, z2_bank).then_inc(z2_turned, 1)
                if t < 2:
                    turn_z2(t, late, zw_bank).then_inc(zw_turned, 1)
            turn_z2(2, range(M2), zw_bank).then_inc(zw_turned, 1)
            pe.wait_ge(sig2_ready, 1)
            turn_z2(3, range(M2), zw_bank).then_inc(zw_turned, 1)
            pe.wait_ge(z2_by_act, M2)
            for t in 2, 3:
                for m in range(M2):
                    last = pe.matmul(plain_sum[:, t:t + 1], z2[:, m, t * P:(t + 1) * P], w3v[:, m:m + 1],
                                     start=(t == 2 and m == 0), stop=(m == M2 - 1), skip_group_check=True)
                last.then_inc(plain_by_pe, 1)


_INS = ['r_items', 'r_users', 'r_history_users', 'L0_rec_item_table', 'L0_rec_user_table', 'L0_rec_W1',
        'L0_rec_b1', 'L0_rec_g1', 'L0_rec_be1', 'L0_rec_a1', 'L0_rec_W2', 'L0_rec_b2', 'L0_rec_g2',
        'L0_rec_be2', 'L0_rec_a2', 'L0_rec_W3', 'L0_rec_b3']


def kernel(**inputs):
    import numpy as np
    import concourse.bacc as bacc
    from concourse.bass_utils import run_bass_kernel_spmd

    nc = bacc.Bacc("TRN2", target_bir_lowering=False, num_devices=1)
    arrays, args = {}, []
    for name in _INS:
        a = np.ascontiguousarray(inputs[name])
        arrays[f"in_{name}"] = a
        args.append(nc.dram_tensor(f"in_{name}", a.shape, mybir.dt.from_np(a.dtype), kind="ExternalInput").ap())
    batch = inputs['r_items'].shape[0]
    args.append(nc.dram_tensor("out", (batch, 1), F32, kind="ExternalOutput").ap())
    recommender_kernel(nc, *args)
    r = run_bass_kernel_spmd(nc, [arrays], core_ids=[0])
    return r.results[0]["out"]
```
